# Optimizing a Trainium2 kernel written in Bass

```python
import numpy as np
import jax
import jax.numpy as jnp

def _softmax(x, axis=-1):
    return jax.nn.softmax(x, axis=axis)

def _gelu(x):
    return jax.nn.gelu(x, approximate=True)

def _silu(x):
    return jax.nn.silu(x)

def _sigmoid(x):
    return jax.nn.sigmoid(x)

def _layernorm(x, axis=-1, eps=1e-05):
    m = jnp.mean(x, axis=axis, keepdims=True)
    v = jnp.var(x, axis=axis, keepdims=True)
    return (x - m) / jnp.sqrt(v + eps)

def _scatter_add(tgt, idx, src, axis=0):
    return tgt.at[idx].add(src)

def _segment_sum(src, seg, n):
    return jax.ops.segment_sum(src, seg, n)
kernel_name = 'mk_perceiver_d1_seqx_r8_eb6347'

def setup_inputs(seed: int=0):
    np.random.seed(seed)
    _w = jnp.asarray

    def _rec_inputs():
        import jax
        import jax.numpy as jnp
        _rk = jax.random.key(seed)
        x = -0.0003929 + 0.9999 * jax.random.normal(jax.random.fold_in(_rk, 1), (2, 128, 256), jnp.float32)
        _lenS = 128 - jax.random.randint(jax.random.fold_in(_rk, 7), (2,), 0, max(1, 128 // 4) + 1, jnp.int32)
        _lenS2 = 2048 - jax.random.randint(jax.random.fold_in(_rk, 8), (2,), 0, max(1, 2048 // 4) + 1, jnp.int32)
        _ctx_1024P = jax.random.normal(jax.random.fold_in(_rk, 11), (2, 16, 128), jnp.float32)
        _ctx_1024c = jax.random.dirichlet(jax.random.fold_in(_rk, 511), 0.3 * jnp.ones((16,), jnp.float32), (2, 2048))
        _ctx_1024t = jnp.einsum('bsk,bkd->bsd', _ctx_1024c, _ctx_1024P)
        _ctx_1024t = _ctx_1024t * jax.lax.rsqrt(jnp.mean(jnp.square(_ctx_1024t)) + 1e-12) * 0.953939
        ctx_1024 = -0.000494167 + 1.00018 * (_ctx_1024t + 0.3 * jax.random.normal(jax.random.fold_in(_rk, 611), (2, 2048, 128), jnp.float32))
        _validS = jnp.arange(128)[None, :] < _lenS[:, None]
        _validS2 = jnp.arange(2048)[None, :] < _lenS2[:, None]
        _causal = jnp.tril(jnp.ones((128, 128), dtype=bool))
        mask_BxS2_bf1 = jnp.ones((2, 2048), dtype=bool)
        return (x, ctx_1024, mask_BxS2_bf1)
    x, ctx_1024, mask_BxS2_bf1 = _rec_inputs()

    def _L0_xattn_setup():
        import jax, jax.numpy as jnp
        import numpy as np
        N_HEADS = 16
        N_KV_HEADS = 8
        HEAD_DIM = 128
        D_TEXT = 256
        D_VISION = 128
        GROUPS = N_HEADS // N_KV_HEADS
        key = jax.random.key(seed)
        ks = jax.random.split(key, 6)
        B, T_text, T_vis = (4, 256, 72)
        text_hidden = jax.random.normal(ks[0], (B, T_text, D_TEXT), dtype=jnp.float32)
        vision_tokens = jax.random.normal(ks[1], (B, T_vis, D_VISION), dtype=jnp.float32)
        vision_mask = jnp.ones((B, T_vis), dtype=bool)
        s = 0.02
        Wq = jax.random.normal(ks[2], (D_TEXT, N_HEADS * HEAD_DIM), dtype=jnp.float32) * s
        Wk = jax.random.normal(ks[3], (D_VISION, N_KV_HEADS * HEAD_DIM), dtype=jnp.float32) * s
        Wv = jax.random.normal(ks[4], (D_VISION, N_KV_HEADS * HEAD_DIM), dtype=jnp.float32) * s
        Wo = jax.random.normal(ks[5], (N_HEADS * HEAD_DIM, D_TEXT), dtype=jnp.float32) * s
        return {'text_hidden': text_hidden, 'vision_tokens': vision_tokens, 'vision_mask': vision_mask, 'Wq': Wq, 'Wk': Wk, 'Wv': Wv, 'Wo': Wo}
    _L0_xattn_all = _L0_xattn_setup()
    _L0_xattn_in = {k: v for k, v in _L0_xattn_all.items() if k in ('Wq', 'Wk', 'Wv', 'Wo')}
    del _L0_xattn_all

    def _L0_attn_setup():
        import jax, jax.numpy as jnp
        import numpy as np
        D_MODEL = 256
        D_STATE = 128
        D_CONV = 4
        EXPAND = 2
        HEADDIM = 64
        NGROUPS = 1
        D_INNER = EXPAND * D_MODEL
        NHEADS = D_INNER // HEADDIM
        D_XBC = D_INNER + 2 * NGROUPS * D_STATE
        D_IN_PROJ = 2 * D_INNER + 2 * NGROUPS * D_STATE + NHEADS
        BLOCK_LEN = 64

        def _segsum(x):
            T = x.shape[-1]
            xc = jnp.cumsum(x, axis=-1)
            seg = xc[..., :, None] - xc[..., None, :]
            mask = jnp.tril(jnp.ones((T, T), dtype=bool))
            return jnp.where(mask, seg, -jnp.inf)

        def _ssd_scan(X, A, B, C, block_len):
            b, L, h, p = X.shape
            c = L // block_len
            X = X.reshape(b, c, block_len, h, p)
            A = A.reshape(b, c, block_len, h).transpose(0, 3, 1, 2)
            B = B.reshape(b, c, block_len, h, -1)
            C = C.reshape(b, c, block_len, h, -1)
            A_cumsum = jnp.cumsum(A, axis=-1)
            Lmat = jnp.exp(_segsum(A))
            Y_diag = jnp.einsum('bclhn,bcshn,bhcls,bcshp->bclhp', C, B, Lmat, X)
            decay_states = jnp.exp(A_cumsum[:, :, :, -1:] - A_cumsum)
            states = jnp.einsum('bclhn,bhcl,bclhp->bchpn', B, decay_states, X)
            init = jnp.zeros_like(states[:, :1])
            states = jnp.concatenate([init, states], axis=1)
            A_last = jnp.pad(A_cumsum[:, :, :, -1], ((0, 0), (0, 0), (1, 0)))
            decay_chunk = jnp.exp(_segsum(A_last))
            new_states = jnp.einsum('bhzc,bchpn->bzhpn', decay_chunk, states)
            states = new_states[:, 1:]
            state_decay_out = jnp.exp(A_cumsum)
            Y_off = jnp.einsum('bclhn,bchpn,bhcl->bclhp', C, states, state_decay_out)
            return (Y_diag + Y_off).reshape(b, L, h, p)

        def _forward(x, in_proj_w, conv_w, conv_b, A_log, D, dt_bias, norm_w, out_proj_w):
            Bsz, L, _ = x.shape
            proj = x @ in_proj_w.T
            z = proj[:, :, :D_INNER]
            xBC = proj[:, :, D_INNER:D_INNER + D_XBC]
            dt_raw = proj[:, :, D_INNER + D_XBC:]
            xBC_t = xBC.transpose(0, 2, 1)
            conv = jax.lax.conv_general_dilated(xBC_t, conv_w, window_strides=(1,), padding=[(D_CONV - 1, 0)], feature_group_count=D_XBC, dimension_numbers=('NCH', 'OIH', 'NCH'))
            conv = conv + conv_b[None, :, None]
            xBC = jax.nn.silu(conv).transpose(0, 2, 1)
            x_ssm = xBC[:, :, :D_INNER]
            B_param = xBC[:, :, D_INNER:D_INNER + NGROUPS * D_STATE]
            C_param = xBC[:, :, D_INNER + NGROUPS * D_STATE:]
            dt = jax.nn.softplus(dt_raw + dt_bias)
            A = -jnp.exp(A_log)
            x_heads = x_ssm.reshape(Bsz, L, NHEADS, HEADDIM)
            hpg = NHEADS // NGROUPS
            X = x_heads * dt[..., None]
            A_disc = dt * A[None, None, :]
            B_heads = jnp.repeat(B_param.reshape(Bsz, L, NGROUPS, D_STATE), hpg, axis=2)
            C_heads = jnp.repeat(C_param.reshape(Bsz, L, NGROUPS, D_STATE), hpg, axis=2)
            pad_len = (BLOCK_LEN - L % BLOCK_LEN) % BLOCK_LEN
            if pad_len > 0:
                X = jnp.pad(X, ((0, 0), (0, pad_len), (0, 0), (0, 0)))
                A_disc = jnp.pad(A_disc, ((0, 0), (0, pad_len), (0, 0)))
                B_heads = jnp.pad(B_heads, ((0, 0), (0, pad_len), (0, 0), (0, 0)))
                C_heads = jnp.pad(C_heads, ((0, 0), (0, pad_len), (0, 0), (0, 0)))
            Y = _ssd_scan(X, A_disc, B_heads, C_heads, BLOCK_LEN)[:, :L]
            Y = Y + x_heads * D[None, None, :, None]
            y = Y.reshape(Bsz, L, D_INNER)
            y = y * jax.nn.silu(z)
            rms = jnp.sqrt(jnp.mean(y * y, axis=-1, keepdims=True) + 1e-05)
            y = y / rms * norm_w
            return y @ out_proj_w.T
        key = jax.random.key(seed)
        ks = jax.random.split(key, 8)
        x = jax.random.normal(ks[0], (2, 256, D_MODEL), dtype=jnp.float32)
        in_proj_w = jax.random.normal(ks[1], (D_IN_PROJ, D_MODEL), dtype=jnp.float32) * 0.02
        conv_w = jax.random.normal(ks[2], (D_XBC, 1, D_CONV), dtype=jnp.float32) * 0.2
        conv_b = jnp.zeros((D_XBC,), dtype=jnp.float32)
        A_log = jnp.log(jnp.arange(1, NHEADS + 1, dtype=jnp.float32))
        D = jnp.ones((NHEADS,), dtype=jnp.float32)
        dt_bias = jax.random.normal(ks[3], (NHEADS,), dtype=jnp.float32) * 0.1
        norm_w = jnp.ones((D_INNER,), dtype=jnp.float32)
        out_proj_w = jax.random.normal(ks[4], (D_MODEL, D_INNER), dtype=jnp.float32) * 0.02
        return {'x': x, 'in_proj_w': in_proj_w, 'conv_w': conv_w, 'conv_b': conv_b, 'A_log': A_log, 'D': D, 'dt_bias': dt_bias, 'norm_w': norm_w, 'out_proj_w': out_proj_w}
    _L0_attn_all = _L0_attn_setup()
    _L0_attn_in = {k: v for k, v in _L0_attn_all.items() if k in ('in_proj_w', 'conv_w', 'conv_b', 'A_log', 'D', 'dt_bias', 'norm_w', 'out_proj_w')}
    del _L0_attn_all

    def _L0_ffn_setup():
        import jax, jax.numpy as jnp
        import numpy as np
        B, T, D, H = (4, 256, 256, 176)
        E, K = (16, 2)
        G, TKG, S = (4, 2, 1)
        SCALE = 1.0

        def _moe(x, gate_w, w1, w2, sw1, sw2):
            Bx, Tx, Dx = x.shape
            xf = x.reshape(-1, Dx)
            N = xf.shape[0]
            shared = jnp.zeros_like(xf)
            for s in range(S):
                shared = shared + jax.nn.silu(xf @ sw1[s]) @ sw2[s]
            scores = jax.nn.sigmoid(xf @ gate_w.T)
            gs = E // G
            sg = scores.reshape(N, G, gs)
            group_scores = jax.lax.top_k(sg, min(2, gs))[0].sum(axis=-1)
            _, gidx = jax.lax.top_k(group_scores, TKG)
            gmask = jax.nn.one_hot(gidx, G, dtype=scores.dtype).max(axis=1)
            masked = (sg * gmask[:, :, None]).reshape(N, E)
            tw, ti = jax.lax.top_k(masked, K)
            tw = tw / (tw.sum(axis=-1, keepdims=True) + 1e-20) * SCALE
            combine = jnp.zeros((N, E), scores.dtype).at[jnp.arange(N)[:, None], ti].add(tw)
            out = shared
            for e in range(E):
                out = out + combine[:, e:e + 1] * (jax.nn.silu(xf @ w1[e]) @ w2[e])
            return out.reshape(Bx, Tx, Dx)
        key = jax.random.key(seed)
        ks = jax.random.split(key, 6)
        x = jax.random.normal(ks[0], (B, T, D), jnp.float32)
        gate_w = jax.random.normal(ks[1], (E, D), jnp.float32) * 0.02
        w1 = jax.random.normal(ks[2], (E, D, H), jnp.float32) * 0.02
        w2 = jax.random.normal(ks[3], (E, H, D), jnp.float32) * 0.02
        sw1 = jax.random.normal(ks[4], (S, D, H), jnp.float32) * 0.02
        sw2 = jax.random.normal(ks[5], (S, H, D), jnp.float32) * 0.02
        return {'x': x, 'gate_w': gate_w, 'w1': w1, 'w2': w2, 'sw1': sw1, 'sw2': sw2}
    _L0_ffn_all = _L0_ffn_setup()
    _L0_ffn_in = {k: v for k, v in _L0_ffn_all.items() if k in ('gate_w', 'w1', 'w2', 'sw1', 'sw2')}
    del _L0_ffn_all
    return {'x': x, 'ctx_1024': ctx_1024, 'mask_BxS2_bf1': mask_BxS2_bf1, 'L0_xattn_Wq': _L0_xattn_in['Wq'], 'L0_xattn_Wk': _L0_xattn_in['Wk'], 'L0_xattn_Wv': _L0_xattn_in['Wv'], 'L0_xattn_Wo': _L0_xattn_in['Wo'], 'L0_attn_in_proj_w': _L0_attn_in['in_proj_w'], 'L0_attn_conv_w': _L0_attn_in['conv_w'], 'L0_attn_conv_b': _L0_attn_in['conv_b'], 'L0_attn_A_log': _L0_attn_in['A_log'], 'L0_attn_D': _L0_attn_in['D'], 'L0_attn_dt_bias': _L0_attn_in['dt_bias'], 'L0_attn_norm_w': _L0_attn_in['norm_w'], 'L0_attn_out_proj_w': _L0_attn_in['out_proj_w'], 'L0_ffn_gate_w': _L0_ffn_in['gate_w'], 'L0_ffn_w1': _L0_ffn_in['w1'], 'L0_ffn_w2': _L0_ffn_in['w2'], 'L0_ffn_sw1': _L0_ffn_in['sw1'], 'L0_ffn_sw2': _L0_ffn_in['sw2']}

def reference(x, ctx_1024, mask_BxS2_bf1, L0_xattn_Wq, L0_xattn_Wk, L0_xattn_Wv, L0_xattn_Wo, L0_attn_in_proj_w, L0_attn_conv_w, L0_attn_conv_b, L0_attn_A_log, L0_attn_D, L0_attn_dt_bias, L0_attn_norm_w, L0_attn_out_proj_w, L0_ffn_gate_w, L0_ffn_w1, L0_ffn_w2, L0_ffn_sw1, L0_ffn_sw2):
    import jax
    import jax.numpy as jnp

    def _L0_xattn_ref(text_hidden, vision_tokens, vision_mask, Wq, Wk, Wv, Wo):
        import jax, jax.numpy as jnp
        import numpy as np
        N_HEADS = 16
        N_KV_HEADS = 8
        HEAD_DIM = 128
        D_TEXT = 256
        D_VISION = 128
        GROUPS = N_HEADS // N_KV_HEADS
        B, T_text, _ = text_hidden.shape
        T_vis = vision_tokens.shape[1]
        scale = jnp.float32(np.sqrt(HEAD_DIM))
        q = (text_hidden @ Wq).reshape(B, T_text, N_HEADS, HEAD_DIM).transpose(0, 2, 1, 3)
        k = (vision_tokens @ Wk).reshape(B, T_vis, N_KV_HEADS, HEAD_DIM).transpose(0, 2, 1, 3)
        v = (vision_tokens @ Wv).reshape(B, T_vis, N_KV_HEADS, HEAD_DIM).transpose(0, 2, 1, 3)
        k = jnp.repeat(k, GROUPS, axis=1)
        v = jnp.repeat(v, GROUPS, axis=1)
        scores = jnp.einsum('bhtd,bhsd->bhts', q, k) / scale
        mask = vision_mask[:, None, None, :]
        scores = jnp.where(mask, scores, -jnp.inf)
        attn = jax.nn.softmax(scores, axis=-1)
        attn = jnp.nan_to_num(attn, nan=0.0)
        out = jnp.einsum('bhts,bhsd->bhtd', attn, v)
        out = out.transpose(0, 2, 1, 3).reshape(B, T_text, N_HEADS * HEAD_DIM)
        return out @ Wo

    def _L0_attn_ref(x, in_proj_w, conv_w, conv_b, A_log, D, dt_bias, norm_w, out_proj_w):
        import jax, jax.numpy as jnp
        import numpy as np
        D_MODEL = 256
        D_STATE = 128
        D_CONV = 4
        EXPAND = 2
        HEADDIM = 64
        NGROUPS = 1
        D_INNER = EXPAND * D_MODEL
        NHEADS = D_INNER // HEADDIM
        D_XBC = D_INNER + 2 * NGROUPS * D_STATE
        D_IN_PROJ = 2 * D_INNER + 2 * NGROUPS * D_STATE + NHEADS
        BLOCK_LEN = 64

        def _segsum(x):
            T = x.shape[-1]
            xc = jnp.cumsum(x, axis=-1)
            seg = xc[..., :, None] - xc[..., None, :]
            mask = jnp.tril(jnp.ones((T, T), dtype=bool))
            return jnp.where(mask, seg, -jnp.inf)

        def _ssd_scan(X, A, B, C, block_len):
            b, L, h, p = X.shape
            c = L // block_len
            X = X.reshape(b, c, block_len, h, p)
            A = A.reshape(b, c, block_len, h).transpose(0, 3, 1, 2)
            B = B.reshape(b, c, block_len, h, -1)
            C = C.reshape(b, c, block_len, h, -1)
            A_cumsum = jnp.cumsum(A, axis=-1)
            Lmat = jnp.exp(_segsum(A))
            Y_diag = jnp.einsum('bclhn,bcshn,bhcls,bcshp->bclhp', C, B, Lmat, X)
            decay_states = jnp.exp(A_cumsum[:, :, :, -1:] - A_cumsum)
            states = jnp.einsum('bclhn,bhcl,bclhp->bchpn', B, decay_states, X)
            init = jnp.zeros_like(states[:, :1])
            states = jnp.concatenate([init, states], axis=1)
            A_last = jnp.pad(A_cumsum[:, :, :, -1], ((0, 0), (0, 0), (1, 0)))
            decay_chunk = jnp.exp(_segsum(A_last))
            new_states = jnp.einsum('bhzc,bchpn->bzhpn', decay_chunk, states)
            states = new_states[:, 1:]
            state_decay_out = jnp.exp(A_cumsum)
            Y_off = jnp.einsum('bclhn,bchpn,bhcl->bclhp', C, states, state_decay_out)
            return (Y_diag + Y_off).reshape(b, L, h, p)

        def _forward(x, in_proj_w, conv_w, conv_b, A_log, D, dt_bias, norm_w, out_proj_w):
            Bsz, L, _ = x.shape
            proj = x @ in_proj_w.T
            z = proj[:, :, :D_INNER]
            xBC = proj[:, :, D_INNER:D_INNER + D_XBC]
            dt_raw = proj[:, :, D_INNER + D_XBC:]
            xBC_t = xBC.transpose(0, 2, 1)
            conv = jax.lax.conv_general_dilated(xBC_t, conv_w, window_strides=(1,), padding=[(D_CONV - 1, 0)], feature_group_count=D_XBC, dimension_numbers=('NCH', 'OIH', 'NCH'))
            conv = conv + conv_b[None, :, None]
            xBC = jax.nn.silu(conv).transpose(0, 2, 1)
            x_ssm = xBC[:, :, :D_INNER]
            B_param = xBC[:, :, D_INNER:D_INNER + NGROUPS * D_STATE]
            C_param = xBC[:, :, D_INNER + NGROUPS * D_STATE:]
            dt = jax.nn.softplus(dt_raw + dt_bias)
            A = -jnp.exp(A_log)
            x_heads = x_ssm.reshape(Bsz, L, NHEADS, HEADDIM)
            hpg = NHEADS // NGROUPS
            X = x_heads * dt[..., None]
            A_disc = dt * A[None, None, :]
            B_heads = jnp.repeat(B_param.reshape(Bsz, L, NGROUPS, D_STATE), hpg, axis=2)
            C_heads = jnp.repeat(C_param.reshape(Bsz, L, NGROUPS, D_STATE), hpg, axis=2)
            pad_len = (BLOCK_LEN - L % BLOCK_LEN) % BLOCK_LEN
            if pad_len > 0:
                X = jnp.pad(X, ((0, 0), (0, pad_len), (0, 0), (0, 0)))
                A_disc = jnp.pad(A_disc, ((0, 0), (0, pad_len), (0, 0)))
                B_heads = jnp.pad(B_heads, ((0, 0), (0, pad_len), (0, 0), (0, 0)))
                C_heads = jnp.pad(C_heads, ((0, 0), (0, pad_len), (0, 0), (0, 0)))
            Y = _ssd_scan(X, A_disc, B_heads, C_heads, BLOCK_LEN)[:, :L]
            Y = Y + x_heads * D[None, None, :, None]
            y = Y.reshape(Bsz, L, D_INNER)
            y = y * jax.nn.silu(z)
            rms = jnp.sqrt(jnp.mean(y * y, axis=-1, keepdims=True) + 1e-05)
            y = y / rms * norm_w
            return y @ out_proj_w.T
        return _forward(x, in_proj_w, conv_w, conv_b, A_log, D, dt_bias, norm_w, out_proj_w)

    def _L0_ffn_ref(x, gate_w, w1, w2, sw1, sw2):
        import jax, jax.numpy as jnp
        import numpy as np
        B, T, D, H = (4, 256, 256, 176)
        E, K = (16, 2)
        G, TKG, S = (4, 2, 1)
        SCALE = 1.0

        def _moe(x, gate_w, w1, w2, sw1, sw2):
            Bx, Tx, Dx = x.shape
            xf = x.reshape(-1, Dx)
            N = xf.shape[0]
            shared = jnp.zeros_like(xf)
            for s in range(S):
                shared = shared + jax.nn.silu(xf @ sw1[s]) @ sw2[s]
            scores = jax.nn.sigmoid(xf @ gate_w.T)
            gs = E // G
            sg = scores.reshape(N, G, gs)
            group_scores = jax.lax.top_k(sg, min(2, gs))[0].sum(axis=-1)
            _, gidx = jax.lax.top_k(group_scores, TKG)
            gmask = jax.nn.one_hot(gidx, G, dtype=scores.dtype).max(axis=1)
            masked = (sg * gmask[:, :, None]).reshape(N, E)
            tw, ti = jax.lax.top_k(masked, K)
            tw = tw / (tw.sum(axis=-1, keepdims=True) + 1e-20) * SCALE
            combine = jnp.zeros((N, E), scores.dtype).at[jnp.arange(N)[:, None], ti].add(tw)
            out = shared
            for e in range(E):
                out = out + combine[:, e:e + 1] * (jax.nn.silu(xf @ w1[e]) @ w2[e])
            return out.reshape(Bx, Tx, Dx)
        return _moe(x, gate_w, w1, w2, sw1, sw2)
    x = x + _L0_xattn_ref(_layernorm(x, axis=-1), ctx_1024, mask_BxS2_bf1, L0_xattn_Wq, L0_xattn_Wk, L0_xattn_Wv, L0_xattn_Wo)
    x = x + _L0_attn_ref(_layernorm(x, axis=-1), L0_attn_in_proj_w, L0_attn_conv_w, L0_attn_conv_b, L0_attn_A_log, L0_attn_D, L0_attn_dt_bias, L0_attn_norm_w, L0_attn_out_proj_w)
    x = x + _L0_ffn_ref(_layernorm(x, axis=-1), L0_ffn_gate_w, L0_ffn_w1, L0_ffn_w2, L0_ffn_sw1, L0_ffn_sw2)
    return x

_drawn_inputs = setup_inputs


def setup_inputs(seed=0):
    import zlib

    import numpy as np

    out = dict(_drawn_inputs(seed))
    spreads = {'L0_attn_conv_b': (0.0, 0.1), 'L0_attn_D': (1.0, 0.2), 'L0_attn_norm_w': (1.0, 0.2)}
    factors = {'L0_xattn_Wq': 8.0, 'L0_xattn_Wk': 8.0, 'L0_attn_A_log': 8.0, 'L0_attn_dt_bias': 8.0}
    for name, (base, spread) in spreads.items():
        noise = np.random.default_rng([zlib.crc32(name.encode()), seed]).standard_normal(out[name].shape)
        drawn = base * np.exp(spread * noise) if base else spread * noise
        out[name] = jnp.asarray(drawn.astype(out[name].dtype))
    for name, factor in factors.items():
        out[name] = (out[name] * factor).astype(out[name].dtype)
    return out
```

```python
from contextlib import ExitStack

import concourse.bass as bass
from concourse import mybir

ALU = mybir.AluOpType
ACT = mybir.ActivationFunctionType
AX_X = mybir.AxisListType.X
F32 = mybir.dt.float32
F32R = mybir.dt.float32r
BF16 = mybir.dt.bfloat16
U8 = mybir.dt.uint8

P = 128
B = 2
D = 256
KT = D // P
S = 2048
ST = S // P
BANK = 512
NB = S // BANK
NKV = 8
SCALE = float(P) ** -0.5
MASKED = -1e30

DI = 512
NH = 8
HD = DI // NH
C = P // 2
NX = 6
NI = 2 * DI + 2 * P + NH
CW = 4

WARM = 20

E = 16
H = 176
NM = 24
G = 4
TPB = 4
PART = 32
W3 = 3 * PART
N_VEC = 2
EPS = 1e-5


def cross_attention_ssm_moe(nc, x, ctx, ctx_t, mask, wqk, wvo, win_t, small_by_row, small_by_head, wout_t, w1, w2,
                            expert_rows, out):
    with ExitStack() as stack:
        def sem(name):
            return stack.enter_context(nc.semaphore(name))

        def psum(name, shape):
            return stack.enter_context(nc.psum_tensor(name, shape, F32))

        def sbuf_in(scope):
            return lambda name, shape, dt=F32: scope.enter_context(nc.sbuf_tensor(name, shape, dt))

        sc_ps = psum("sc_ps", [P, NB, BANK])
        tr_ps = psum("tr_ps", [P, 2, BANK])
        pv_ps = psum("pv_ps", [P, BANK])
        misc_ps = psum("misc_ps", [P, BANK])

        keep = sbuf_in(stack)
        x_sb = keep("x_sb", [P, B, D])
        x1 = keep("x1", [P, B, D])
        ident = keep("ident", [P, P])
        after = keep("after", [P, P])
        after_in = keep("after_in", [P, P])
        upto = keep("upto", [P, P])
        upto_c = keep("upto_c", [P, C])
        win = keep("win", [P, KT, NI])
        wout = keep("wout", [P, DI // P, D])
        by_row = keep("by_row", [P, NX * CW + NX + DI // P + KT * E])
        by_head = keep("by_head", [P, 3, NH])
        a_rate = keep("a_rate", [P, NH])
        w1_sb = keep("w1_sb", [P, TPB, KT, P])
        w2_sb = keep("w2_sb", [P, TPB, D])
        any_valid = keep("any_valid", [P, B])
        stats = keep("stats", [P, B, 6])
        mv = keep("mv", [P, B, 2])
        vare = keep("vare", [P, B])
        rstd = keep("rstd", [P, B])
        mhalf = keep("mhalf", [P, B])

        attn = ExitStack()
        with ExitStack() as staging:
            ctxT_raw = [sbuf_in(staging)(f"ctxT_raw{b}", [P, S]) for b in range(B)]
            ctx_raw = [sbuf_in(staging)(f"ctx_raw{b}", [P, ST, P]) for b in range(B)]
            mask_u8 = sbuf_in(staging)("mask_u8", [P, B, S], U8)
        a_sb = sbuf_in(attn)
        pt = [None, None]
        pt[1] = a_sb("pt1", [P, ST, BANK], F32R)
        pt[0] = a_sb("pt0", [P, ST, BANK], F32R)
        ctxT_hi = [a_sb(f"ctxT_hi{b}", [P, S], F32R) for b in range(B)]
        ctxT_lo = [a_sb(f"ctxT_lo{b}", [P, S], F32R) for b in range(B)]
        ctx_hi = [a_sb(f"ctx_hi{b}", [P, ST, P], F32R) for b in range(B)]
        ctx_lo = [a_sb(f"ctx_lo{b}", [P, ST, P], F32R) for b in range(B)]
        probs = a_sb("probs", [P, 2, S])
        pen = a_sb("pen", [P, B, S], BF16)
        wqk_sb = a_sb("wqk_sb", [P, KT * 2 * P + P])
        wvo_sb = a_sb("wvo_sb", [P, P + 2 * D])
        xn = a_sb("xn", [P, B, D])
        xnT = a_sb("xnT", [P, KT, B * P])
        qT = a_sb("qT", [P, 2, B * P])
        qk_hi = a_sb("qk_hi", [P, 2 * B * P], F32R)
        qk_lo = a_sb("qk_lo", [P, 2 * B * P], F32R)
        wvo_h = a_sb("wvo_h", [P, 2, D])
        outT = a_sb("outT", [P, 2 * P])
        yacc = a_sb("yacc", [P, B, D])
        mx = a_sb("mx", [P, 2, NB])
        taker = a_sb("taker", [P, NB])
        nmax = a_sb("nmax", [P, 2])
        zsum = a_sb("zsum", [P, 4])
        rz = a_sb("rz", [P, 2, 2])
        attn.close()

        late = ExitStack()
        l_sb = sbuf_in(late)
        xn2 = l_sb("xn2", [P, B, D])
        x2T = l_sb("x2T", [P, KT, B * P])
        conv = l_sb("conv", [P, NX, B, P])
        xc = l_sb("xc", [P, NX, B, P])
        dtv = l_sb("dtv", [P, 14, B, NH])
        dt = l_sb("dt", [P, B, NH])
        a_dt = l_sb("a_dt", [P, B, NH])
        ends = l_sb("ends", [P, 3, B, NH])
        steps = l_sb("steps", [P, B, NH, C])
        decay = l_sb("decay", [P, B, NH, C])
        bc = l_sb("bc", [P, B, P])
        bc_in = l_sb("bc_in", [P, B, P])
        mT = l_sb("mT", [P, B, NH, P])
        xdt = l_sb("xdt", [P, B, NH, HD])
        xd = l_sb("xd", [P, B, NH, HD])
        xq = l_sb("xq", [P, B, 2, NH, HD])
        y_off = l_sb("y_off", [P, B, NH, HD])
        y_add = l_sb("y_add", [P, B, NH, HD])
        sz = l_sb("sz", [P, B, DI])
        y1 = l_sb("y1", [P, B, DI])
        y2 = l_sb("y2", [P, B, DI])
        ysq = l_sb("ysq", [P, B, DI])
        ss = l_sb("ss", [P, B])
        sse = l_sb("sse", [P, B])
        rinv = l_sb("rinv", [P, B])
        yT = l_sb("yT", [P, B, DI // P, P])
        x2 = l_sb("x2", [P, B, D])
        xn3 = l_sb("xn3", [P, B, D])
        x3T = l_sb("x3T", [P, KT, B * P])
        sg = l_sb("sg", [P, B, E])
        pairs = l_sb("pairs", [P, B * G, 6])
        gsum = l_sb("gsum", [P, B, G])
        low_g = l_sb("low_g", [P, G, G])
        low_e = l_sb("low_e", [P, E, E])
        cmp_g = l_sb("cmp_g", [P, 3, B, G, G])
        rank_g = l_sb("rank_g", [P, B, G])
        sel_g = l_sb("sel_g", [P, B, G])
        cand = l_sb("cand", [P, B, E])
        cmp_e = l_sb("cmp_e", [P, 3, B, E, E])
        rank_e = l_sb("rank_e", [P, B, E])
        sel_e = l_sb("sel_e", [P, B, E])
        wsel = l_sb("wsel", [P, B, E])
        wsum = l_sb("wsum", [P, B])
        wrec = l_sb("wrec", [P, B])
        comb = l_sb("comb", [P, B, E])
        comb_hi = l_sb("comb_hi", [P, B, E], BF16)
        comb_rest = l_sb("comb_rest", [P, B, E])
        comb_mid = l_sb("comb_mid", [P, B, E], BF16)
        comb3 = l_sb("comb3", [P, B, W3])
        comb3T = l_sb("comb3T", [W3, B * P], BF16)
        rows = l_sb("rows", [W3, NM * P], BF16)
        hs = l_sb("hs", [P, 4, B * P])
        hc = l_sb("hc", [P, 4, B * P])
        res = l_sb("res", [P, B, D])
        late.close()

        cut = [0, NX * CW, NX * CW + NX, NX * CW + NX + DI // P, NX * CW + NX + DI // P + KT * E]
        convw = by_row[:, cut[0]:cut[1]].rearrange("p (j w) -> p j w", w=CW)
        convb, normw = by_row[:, cut[1]:cut[2]], by_row[:, cut[2]:cut[3]]
        gate = by_row[:, cut[3]:cut[4]].rearrange("p (k e) -> p k e", e=E)
        alog, dskip, dtb = (by_head[:, k] for k in range(3))

        x_in, mask_in, vec_in, rows_in = sem("x_in"), sem("mask_in"), sem("vec_in"), sem("rows_in")
        ctxT_in = [sem(f"ctxT_in{b}") for b in range(B)]
        ctx_in = [sem(f"ctx_in{b}") for b in range(B)]
        wqk_in, wvo_in, win_in, wout_in = sem("wqk_in"), sem("wvo_in"), sem("win_in"), sem("wout_in")
        w1_in = [sem(f"w1_in{k}") for k in range(TPB)]
        w2_in = [sem(f"w2_in{k}") for k in range(TPB)]
        out_sent = sem("out_sent")

        const_set, const_ok, split_hi, split_lo = sem("const_set"), sem("const_ok"), sem("split_hi"), sem("split_lo")
        split_T0, pen_ok, any_ok, wout_ok = sem("split_T0"), sem("pen_ok"), sem("any_ok"), sem("wout_ok")
        ahead_exp = sem("ahead_exp")
        bn_done, mv_ok, var_ok, rstd_ok = sem("bn_done"), sem("mv_ok"), sem("var_ok"), sem("rstd_ok")
        xn_ok, xnT_ps, xnT_ok = sem("xn_ok"), sem("xnT_ps"), sem("xnT_ok")
        scores, masked, negmax, exps = sem("scores"), sem("masked"), sem("negmax"), sem("exps")
        turned, turned_hi, turned_lo = sem("turned"), sem("turned_hi"), sem("turned_lo")
        pv, outT_ok = sem("pv"), sem("outT_ok")
        q_ps, q_ok, qk_ps, qkhi_ok, qk_ok = sem("q_ps"), sem("q_ok"), sem("qk_ps"), sem("qkhi_ok"), sem("qk_ok")
        wvo_ps, wvo_ok, y_ps, y_ok, recips = sem("wvo_ps"), sem("wvo_ok"), sem("y_ps"), sem("y_ok"), sem("recips")
        x1_ok = sem("x1_ok")
        dt_ps, dt_abs, dt_exp, dt_one, dt_ln, a_ok = sem("dt_ps"), sem("dt_abs"), sem("dt_exp"), sem("dt_one"), sem("dt_ln"), sem("a_ok")
        xbc_ps, tap0, taps, xc_ok, z_ps, sz_ok = sem("xbc_ps"), sem("tap0"), sem("taps"), sem("xc_ok"), sem("z_ps"), sem("sz_ok")
        steps0_ok, steps1_ok, seg_ps, decay_ok = sem("steps0_ok"), sem("steps1_ok"), sem("seg_ps"), sem("decay_ok")
        ends_ps, ends_ok, xq_ok, off_ps = sem("ends_ps"), sem("ends_ok"), sem("xq_ok"), sem("off_ps")
        g_ps, bc_ok, bcin_ok, xh_ps, xdt_ok, mT_ok = sem("g_ps"), sem("bc_ok"), sem("bcin_ok"), sem("xh_ps"), sem("xdt_ok"), sem("mT_ok")
        ssm_ps, y2_ok, sq_ok, ss_ok, rinv_ok = sem("ssm_ps"), sem("y2_ok"), sem("sq_ok"), sem("ss_ok"), sem("rinv_ok")
        yT_ps, yT_ok, o_ps, x2_ok = sem("yT_ps"), sem("yT_ok"), sem("o_ps"), sem("x2_ok")
        dve_step = sem("dve_step")
        order_set, order_ok = sem("order_set"), sem("order_ok")
        gate_ps, sg_ok, comb_ok, combT_ps, combT_ok = sem("gate_ps"), sem("sg_ok"), sem("comb_ok"), sem("combT_ps"), sem("combT_ok")
        h_ps, c_ps, h_act, h_ok, h_used, res_ok = sem("h_ps"), sem("c_ps"), sem("h_act"), sem("h_ok"), sem("h_used"), sem("res_ok")

        block = stack.enter_context(nc.Block())

        @block.sync
        def _(sp):
            sp.dma_start(x_sb[:], x.rearrange("b t d -> t b d")).then_inc(x_in, 16)
            sp.dma_start(ctxT_raw[0][:], ctx_t[0]).then_inc(ctxT_in[0], 16)
            sp.dma_start(mask_u8[:], mask.partition_broadcast(P)).then_inc(mask_in, 16)
            sp.dma_start(ctxT_raw[1][:], ctx_t[1]).then_inc(ctxT_in[1], 16)
            for b in range(B):
                sp.dma_start(ctx_raw[b][:], ctx[b].rearrange("(n p) v -> p n v", p=P)).then_inc(ctx_in[b], 16)
            sp.dma_start(wvo_sb[:], wvo[0]).then_inc(wvo_in, 16)
            sp.dma_start(by_row[:], small_by_row).then_inc(vec_in, 16)
            sp.dma_start(by_head[:].rearrange("p k h -> p (k h)"), small_by_head.partition_broadcast(P)).then_inc(vec_in, 16)
            sp.wait_ge(qk_ps, 1)
            sp.dma_start(wqk_sb[:], wqk[1]).then_inc(wqk_in, 16)
            sp.dma_start(win[:], win_t.rearrange("(k p) n -> p k n", p=P)).then_inc(win_in, 16)
            sp.dma_start(wout[:], wout_t.rearrange("(j p) n -> p j n", p=P)).then_inc(wout_in, 16)
            for k in range(TPB):
                sp.dma_start(w1_sb[:, k], w1[k]).then_inc(w1_in[k], 16)
                sp.dma_start(w2_sb[:, k], w2[k]).then_inc(w2_in[k], 16)
            with sp.Fori(1, NKV - 1) as i:
                sp.wait_ge(wvo_ps, i)
                sp.dma_start(wvo_sb[:], wvo[i]).then_inc(wvo_in, 16)
                sp.wait_ge(qk_ps, i + 1)
                sp.dma_start(wqk_sb[:], wqk[i + 1]).then_inc(wqk_in, 16)
            sp.wait_ge(wvo_ps, NKV - 1)
            sp.dma_start(wvo_sb[:], wvo[NKV - 1]).then_inc(wvo_in, 16)
            sp.wait_ge(x1_ok, B)
            sp.dma_start(rows[:], expert_rows.bitcast(BF16)).then_inc(rows_in, 16)

            def refill(r, first):
                for k in range(TPB):
                    sp.wait_ge(h_ps, TPB * r + (k + 1 - TPB))
                    sp.dma_start(w1_sb[:, k], w1[TPB * r + k]).then_inc(w1_in[k], 16)
                    if k >= 2 or not first:
                        k2 = (k + 2) % TPB
                        sp.wait_ge(h_used, TPB * r + (k - 1 - TPB))
                        sp.dma_start(w2_sb[:, k2], w2[TPB * r + (k - 2)]).then_inc(w2_in[k2], 16)

            refill(1, True)
            with sp.Fori(2, NM // TPB) as r:
                refill(r, False)
            for k2 in (2, 3):
                sp.wait_ge(h_used, NM - 2 * TPB + k2 + 1)
                sp.dma_start(w2_sb[:, k2], w2[NM - TPB + k2]).then_inc(w2_in[k2], 16)
            for b in range(B):
                sp.wait_ge(res_ok, b + 1)
                sp.dma_start(out[b], res[:, b]).then_inc(out_sent, 16)
            sp.wait_ge(out_sent, 16 * B)

        @block.gpsimd
        def _(pool):
            pool.memset(ident[:], 1.0).then_inc(const_set, 1)
            pool.memset(mhalf[:], -0.5).then_inc(const_set, 1)
            for tri in (after, after_in, upto):
                pool.memset(tri[:], 1.0).then_inc(const_set, 1)
            pool.memset(upto_c[:], 1.0).then_inc(const_set, 1)
            pool.wait_ge(const_set, 6)
            pool.affine_select(out=ident[:], in_=ident[:], compare_op=ALU.is_equal, fill=0.0, base=0,
                               pattern=[[-1, P]], channel_multiplier=1).then_inc(const_ok, 1)
            pool.wait_ge(var_ok, 1)
            pool.tensor_tensor(rstd[:], vare[:], mhalf[:], ALU.pow).then_inc(rstd_ok, 1)
            pool.wait_ge(split_hi, 1)
            pool.tensor_tensor(ctxT_lo[1][:], ctxT_raw[1][:], ctxT_hi[1][:].bitcast(F32), ALU.subtract).then_inc(split_lo, 1)
            for b in range(B):
                pool.wait_ge(split_hi, b + 2)
                pool.tensor_tensor(ctx_lo[b][:], ctx_raw[b][:], ctx_hi[b][:].bitcast(F32), ALU.subtract).then_inc(split_lo, 1)
            for tri in (after, after_in):
                pool.affine_select(out=tri[:], in_=tri[:], compare_op=ALU.is_gt, fill=0.0, base=0,
                                   pattern=[[-1, P]], channel_multiplier=1).then_inc(const_ok, 1)
            pool.affine_select(out=upto[:], in_=upto[:], compare_op=ALU.is_ge, fill=0.0, base=0,
                               pattern=[[1, P]], channel_multiplier=-1).then_inc(const_ok, 1)
            for c in range(2):
                half = upto_c[c * C:(c + 1) * C]
                pool.wait_ge(const_ok, 4 + c)
                pool.affine_select(out=half, in_=half, compare_op=ALU.is_ge, fill=0.0, base=0,
                                   pattern=[[1, C]], channel_multiplier=-1).then_inc(const_ok, 1)
            pool.wait_ge(const_ok, 6)
            pool.memset(after_in[C:P, 0:C], 0.0).then_inc(const_ok, 1)
            pool.wait_ge(const_ok, 7)
            pool.memset(upto[0:C, C:P], 0.0).then_inc(const_ok, 1)
            pool.wait_ge(const_ok, 8)
            pool.wait_ge(vec_in, 16 * N_VEC)
            pool.wait_ge(wout_in, 16)
            for j in range(DI // P):
                pool.tensor_scalar(wout[:, j], wout[:, j], normw[:, j:j + 1], 1.0, ALU.mult, ALU.mult).then_inc(wout_ok, 1)

            pool.wait_ge(x1_ok, B)
            pool.wait_ge(var_ok, 2)
            pool.tensor_tensor(rstd[:], vare[:], mhalf[:], ALU.pow).then_inc(rstd_ok, 1)
            pool.memset(low_g[:], 1.0).then_inc(order_set, 1)
            pool.memset(low_e[:], 1.0).then_inc(order_set, 1)
            pool.memset(comb3[:], 0.0).then_inc(order_set, 1)
            pool.wait_ge(a_ok, 1)
            pool.tensor_tensor(steps[:, 1], a_dt[:, 1].unsqueeze(2).broadcast_to([P, NH, C]),
                               upto_c[:].unsqueeze(1).broadcast_to([P, NH, C]), ALU.mult).then_inc(steps1_ok, 1)
            pool.wait_ge(order_set, 3)
            pool.memset(comb3[:, :, E], 1.0).then_inc(order_ok, 1)
            pool.affine_select(out=low_g[:], in_=low_g[:], compare_op=ALU.is_gt, fill=0.0, base=0,
                               pattern=[[1, G], [-1, G]], channel_multiplier=0).then_inc(order_ok, 1)
            pool.affine_select(out=low_e[:], in_=low_e[:], compare_op=ALU.is_gt, fill=0.0, base=0,
                               pattern=[[1, E], [-1, E]], channel_multiplier=0).then_inc(order_ok, 1)
            pool.wait_ge(ends_ok, 1)
            for b in range(B):
                pool.wait_ge(xdt_ok, b + 1)
                for c in range(2):
                    rows_c = slice(0, (c + 1) * C)
                    pool.tensor_tensor(xq[rows_c, b, c], xdt[rows_c, b],
                                       ends[rows_c, 1 - c, b].unsqueeze(2).broadcast_to([(c + 1) * C, NH, HD]),
                                       ALU.mult).then_inc(xq_ok, 1)
            pool.wait_ge(ss_ok, 1)
            pool.tensor_tensor(rinv[:], sse[:], mhalf[:], ALU.pow).then_inc(rinv_ok, 1)
            pool.wait_ge(var_ok, 3)
            pool.tensor_tensor(rstd[:], vare[:], mhalf[:], ALU.pow).then_inc(rstd_ok, 1)

        def pair_of(u):
            return u // 2

        @block.tensor
        def _(pe):
            def turn_tokens(src, done):
                for k in range(KT):
                    for b in range(B):
                        last = nc.tensor.transpose(tr_ps[:, 0, (k * B + b) * P:(k * B + b + 1) * P],
                                                   src[:, b, k * P:(k + 1) * P], ident[:])
                last.then_inc(done, 1)

            def project_q():
                for h in range(2):
                    for k in range(KT):
                        last = nc.tensor.matmul(misc_ps[:, h * B * P:(h + 1) * B * P],
                                                wqk_sb[:, k * 2 * P + h * P:k * 2 * P + (h + 1) * P], xnT[:, k],
                                                start=(k == 0), stop=(k == KT - 1))
                last.then_inc(q_ps, 1)

            def fold_k():
                nc.tensor.matmul(misc_ps[:], wqk_sb[:, KT * 2 * P:], qT[:].rearrange("p h t -> p (h t)"),
                                 start=True, stop=True).then_inc(qk_ps, 1)

            def fold_v():
                nc.tensor.matmul(misc_ps[:], wvo_sb[:, 0:P], wvo_sb[:, P:], start=True, stop=True).then_inc(wvo_ps, 1)

            def unit_scores(n, b, h, first):
                cols = slice(h * B * P + b * P, h * B * P + (b + 1) * P)
                for j in range(NB):
                    if not first:
                        pe.wait_ge(masked, 4 * n + (j - 3))
                    js = slice(j * BANK, (j + 1) * BANK)
                    nc.tensor.matmul(sc_ps[:, j], qk_hi[:, cols], ctxT_hi[b][:, js], start=True, stop=False)
                    nc.tensor.matmul(sc_ps[:, j], qk_hi[:, cols], ctxT_lo[b][:, js], start=False, stop=False)
                    nc.tensor.matmul(sc_ps[:, j], qk_lo[:, cols], ctxT_hi[b][:, js],
                                     start=False, stop=True).then_inc(scores, 1)

            def turn_probs(m, mu, g, first):
                if g == 0:
                    pe.wait_ge(exps, m + 1)
                if not (first and g < 2):
                    pe.wait_ge(turned_lo, 4 * m + (g - 1))
                for s in range(4):
                    t = 4 * g + s
                    last = nc.tensor.transpose(tr_ps[:, g % 2, s * P:(s + 1) * P],
                                               probs[:, mu % 2, t * P:(t + 1) * P], ident[:])
                last.then_inc(turned, 1)

            def pair_pv(pp, t):
                nc.tensor.matmul(pv_ps[:], ctx_hi[pp][:, t], pt[pp][:, t], start=(t == 0), stop=False)
                last = nc.tensor.matmul(pv_ps[:, 0:2 * P], ctx_lo[pp][:, t], pt[pp][:, t, 0:2 * P],
                                        start=False, stop=(t == ST - 1))
                if t == ST - 1:
                    last.then_inc(pv, 1)

            def pair_y():
                for h in range(2):
                    last = nc.tensor.matmul(misc_ps[:, h * D:(h + 1) * D], outT[:, h * P:(h + 1) * P], wvo_h[:, h],
                                            start=True, stop=True)
                last.then_inc(y_ps, 1)

            def iteration(i, prev, more):
                for u in range(4):
                    n, b, h = 4 * i + u, u // 2, u % 2
                    if u == 0:
                        pe.wait_ge(qk_ok, i + 1)
                    if not prev and u == 0:
                        pe.wait_ge(split_T0, 2)
                    if not prev and u == 2:
                        pe.wait_ge(split_hi, 1)
                        pe.wait_ge(split_lo, 1)
                    unit_scores(n, b, h, not prev and u == 0)
                    if u == 0 and prev:
                        pe.wait_ge(wvo_in, 16 * i)
                        pe.wait_ge(qk_ok, i + 1)
                        pe.wait_ge(y_ok, 4 * i - 3)
                        fold_v()
                    if u == 1 and prev:
                        pe.wait_ge(wvo_ok, i)
                        pe.wait_ge(outT_ok, 2 * i - 1)
                        pair_y()
                    if u == 2 and more:
                        pe.wait_ge(wqk_in, 16 * i + 32)
                        if prev:
                            pe.wait_ge(y_ok, 4 * i - 1)
                        project_q()
                    if u == 3 and more:
                        pe.wait_ge(q_ok, i + 2)
                        fold_k()
                    for g in range(4):
                        if prev or u > 0:
                            turn_probs(n - 1, (u + 3) % 4, g, not prev and u == 1)
                        if g == 0 and u == 3:
                            pe.wait_ge(turned_lo, 16 * i + 8)
                            if prev:
                                pe.wait_ge(outT_ok, 2 * i)
                            else:
                                pe.wait_ge(split_lo, 2)
                                pe.wait_ge(split_hi, 2)
                        if g == 0 and u == 1 and prev:
                            pe.wait_ge(turned_lo, 16 * i)
                            pe.wait_ge(outT_ok, 2 * i - 1)
                            pe.wait_ge(split_lo, 3)
                        for t in (2 * g, 2 * g + 1):
                            if u == 3:
                                pair_pv(0, t)
                            elif prev:
                                pair_pv(*((0, t + 8), (1, t), (1, t + 8))[u])
                        if g == 2 and u == 3 and prev:
                            pe.wait_ge(outT_ok, 2 * i)
                            if more:
                                pe.wait_ge(qk_ok, i + 2)
                            else:
                                pe.wait_ge(y_ok, 4 * i - 1)
                            pair_y()

            pe.wait_ge(const_ok, 1)
            for n in range(WARM):
                nc.tensor.transpose(tr_ps[:, 1, 0:P], ident[:], ident[:])
            pe.wait_ge(xn_ok, B)
            turn_tokens(xn, xnT_ps)
            pe.wait_ge(xnT_ok, 1)
            pe.wait_ge(wqk_in, 16)
            project_q()
            pe.wait_ge(q_ok, 1)
            fold_k()
            iteration(0, False, True)
            with pe.Fori(1, NKV - 1) as i:
                iteration(i, True, True)
            iteration(NKV - 1, True, False)
            pe.wait_ge(wvo_in, 16 * NKV)
            pe.wait_ge(y_ok, 4 * NKV - 3)
            fold_v()
            for g in range(4):
                turn_probs(4 * NKV - 1, 3, g, False)
                pair_pv(0, 8 + 2 * g)
                pair_pv(0, 9 + 2 * g)
            pe.wait_ge(wvo_ok, NKV)
            pe.wait_ge(outT_ok, 2 * NKV - 1)
            pair_y()
            pe.wait_ge(turned_lo, 16 * NKV)
            for t in range(ST):
                pair_pv(1, t)
            pe.wait_ge(outT_ok, 2 * NKV)
            pe.wait_ge(y_ok, 4 * NKV - 1)
            pair_y()

            pe.wait_ge(xn_ok, 2 * B)
            turn_tokens(xn2, xnT_ps)
            pe.wait_ge(xnT_ok, 2)
            pe.wait_ge(win_in, 16)
            for b in range(B):
                for k in range(KT):
                    last = nc.tensor.matmul(misc_ps[:, b * NH:(b + 1) * NH], x2T[:, k, b * P:(b + 1) * P],
                                            win[:, k, NI - NH:], start=(k == 0), stop=(k == KT - 1))
            last.then_inc(dt_ps, 1)
            for c in (2, 0, 1):
                for j in (2 * c, 2 * c + 1):
                    for k in range(KT):
                        last = nc.tensor.matmul(sc_ps[:, c, (j % 2) * B * P:(j % 2 + 1) * B * P],
                                                win[:, k, DI + j * P:DI + (j + 1) * P], x2T[:, k],
                                                start=(k == 0), stop=(k == KT - 1))
                last.then_inc(xbc_ps, 1)
            for b in range(B):
                for k in range(KT):
                    last = nc.tensor.matmul(sc_ps[:, 3] if b == 0 else pv_ps[:], x2T[:, k, b * P:(b + 1) * P],
                                            win[:, k, 0:DI], start=(k == 0), stop=(k == KT - 1))
                last.then_inc(z_ps, 1)
                if b == 0:
                    pe.wait_ge(const_ok, 8)
                    pe.wait_ge(a_ok, 1)
                    for k, tri in enumerate((after, after_in, upto)):
                        last = nc.tensor.matmul(tr_ps[:, 1, k * B * NH:(k + 1) * B * NH], tri[:],
                                                a_dt[:].rearrange("p b h -> p (b h)"), start=True, stop=True)
                    last.then_inc(ends_ps, 1)
                    pe.wait_ge(steps0_ok, 1)
                else:
                    pe.wait_ge(steps1_ok, 1)
                    pe.wait_ge(ends_ok, 1)
                nc.tensor.matmul(tr_ps[:, b], after_in[:], steps[:, b].rearrange("p h t -> p (h t)"),
                                 start=True, stop=True).then_inc(seg_ps, 1)
            pe.wait_ge(xc_ok, 1)
            pe.wait_ge(dt_abs, 1)
            for b in range(B):
                last = nc.tensor.matmul(misc_ps[:, b * P:(b + 1) * P], xc[:, 4, b], xc[:, 5, b], start=True, stop=True)
            last.then_inc(g_ps, 1)
            pe.wait_ge(xc_ok, 3)
            for b in range(B):
                for j in range(4):
                    last = nc.tensor.transpose(sc_ps[:, b, j * P:(j + 1) * P], xc[:, j, b], ident[:])
                last.then_inc(xh_ps, 1)
            for b in range(B):
                pe.wait_ge(bc_ok, 1)
                pe.wait_ge(sz_ok, b + 1)
                for c in range(2):
                    pe.wait_ge(xq_ok, 2 * b + c + 1)
                    rows_c = slice(0, (c + 1) * C)
                    last = nc.tensor.matmul((sc_ps[:, 3] if b == 0 else pv_ps[:])[c * C:(c + 1) * C],
                                            bc[rows_c, b, c * C:(c + 1) * C],
                                            xq[rows_c, b, c].rearrange("p h d -> p (h d)"), start=True, stop=True)
                last.then_inc(off_ps, 1)
                pe.wait_ge(mT_ok, b + 1)
                for h in range(NH):
                    last = nc.tensor.matmul((sc_ps[:, 2] if b == 0 else misc_ps[:])[:, h * HD:(h + 1) * HD], mT[:, b, h], xdt[:, b, h],
                                            start=True, stop=True)
                last.then_inc(ssm_ps, 1)
            for b in range(B):
                pe.wait_ge(y2_ok, b + 1)
                if b == 0:
                    pe.wait_ge(decay_ok, 2)
                for j in range(DI // P):
                    last = nc.tensor.transpose(tr_ps[:, b, j * P:(j + 1) * P], y2[:, b, j * P:(j + 1) * P], ident[:])
                last.then_inc(yT_ps, 1)
            pe.wait_ge(wout_ok, DI // P)
            for b in range(B):
                pe.wait_ge(yT_ok, b + 1)
                for j in range(DI // P):
                    last = nc.tensor.matmul(sc_ps[:, b, 0:D], yT[:, b, j], wout[:, j], start=(j == 0), stop=(j == DI // P - 1))
                last.then_inc(o_ps, 1)

            pe.wait_ge(xn_ok, 3 * B)
            turn_tokens(xn3, xnT_ps)
            pe.wait_ge(xnT_ok, 3)
            pe.wait_ge(vec_in, 16 * N_VEC)
            for b in range(B):
                for k in range(KT):
                    last = nc.tensor.matmul(pv_ps[:, b * E:(b + 1) * E], x3T[:, k, b * P:(b + 1) * P], gate[:, k],
                                            start=(k == 0), stop=(k == KT - 1))
            last.then_inc(gate_ps, 1)

            def hidden(r, k):
                pe.wait_ge(w1_in[k], 16 * r + 16)
                for kt in range(KT):
                    last = nc.tensor.matmul(sc_ps[:, k, 0:B * P], w1_sb[:, k, kt], x3T[:, kt],
                                            start=(kt == 0), stop=(kt == KT - 1))
                last.then_inc(h_ps, 1)

            def expert_tile(m, r, k, first):
                if not first:
                    pe.wait_ge(h_act, m - 3)
                    hidden(r, k)
                if k >= 2 or not first:
                    pe.wait_ge(h_ok, m - 1)
                nc.tensor.matmul(tr_ps[:, k % 2, 0:B * P], rows[:, bass.ds(m * P, P)], comb3T[:],
                                 start=True, stop=True).then_inc(c_ps, 1)
                if k >= 2 or not first:
                    expert_out(r if k >= 2 else r - 1, (k + 2) % TPB, first and k == 2, False)

            def expert_out(r, k, begins, ends):
                pe.wait_ge(w2_in[k], 16 * r + 16)
                for b in range(B):
                    last = nc.tensor.matmul((pv_ps if b == 0 else misc_ps)[:, 0:D], hc[:, k, b * P:(b + 1) * P], w2_sb[:, k],
                                            start=begins, stop=ends)
                last.then_inc(h_used, 1)

            for k in range(TPB):
                if k < 2:
                    pe.wait_ge(x2_ok, B)
                hidden(0, k)
            pe.wait_ge(comb_ok, 1)
            for b in range(B):
                last = nc.tensor.transpose(misc_ps[0:W3, b * P:(b + 1) * P], comb3[:, b], ident[:])
            last.then_inc(combT_ps, 1)
            pe.wait_ge(combT_ok, 1)
            pe.wait_ge(rows_in, 16)
            for k in range(TPB):
                expert_tile(k, 0, k, True)
            with pe.Fori(1, NM // TPB) as r:
                for k in range(TPB):
                    expert_tile(TPB * r + k, r, k, False)
            for k in (2, 3):
                pe.wait_ge(h_ok, NM - TPB + k + 1)
                expert_out(NM // TPB - 1, k, False, k == 3)

        @block.scalar
        def _(act):
            def split_high(dst, src, arrived):
                act.wait_ge(arrived, 16)
                nc.scalar.copy(dst[:], src[:]).then_inc(split_hi, 1)

            def iteration(i, prev, more):
                for u in range(4):
                    n = 4 * i + u
                    if u == 0 and prev:
                        act.wait_ge(wvo_ps, i)
                        nc.scalar.copy(wvo_h[:].rearrange("p h d -> p (h d)"), misc_ps[:]).then_inc(wvo_ok, 1)
                    if u == 2 and more:
                        act.wait_ge(q_ps, i + 2)
                        nc.scalar.copy(qT[:].rearrange("p h t -> p (h t)"), misc_ps[:]).then_inc(q_ok, 1)
                    if u == 3 and more:
                        act.wait_ge(qk_ps, i + 2)
                        nc.scalar.copy(qk_hi[:], misc_ps[:]).then_inc(qkhi_ok, 1)
                    if u == 1 and prev:
                        act.wait_ge(pv, 2 * i - 1)
                    if u == 3 and prev:
                        act.wait_ge(pv, 2 * i)
                    if u == 1 and not prev:
                        act.wait_ge(pen_ok, B)
                    if u == 3 and not prev:
                        act.wait_ge(split_lo, 3)
                        act.wait_ge(split_T0, 2)
                    if prev or u > 0:
                        high_parts(n - 1, (u + 3) % 4)
                    if not prev and u == 0:
                        split_high(ctxT_hi[1], ctxT_raw[1], ctxT_in[1])
                    exponentials(n, u)
                    if not prev and u < 2:
                        split_high(ctx_hi[u], ctx_raw[u], ctx_in[u])

            def high_parts(m, mu):
                for g in range(4):
                    act.wait_ge(turned, 4 * m + (g + 1))
                    nc.scalar.copy(pt[mu // 2][:, 4 * g:4 * g + 4, (mu % 2) * P:(mu % 2 + 1) * P],
                                   tr_ps[:, g % 2].rearrange("p (s t) -> p s t", s=4)).then_inc(turned_hi, 1)

            def exponentials(n, u):
                act.wait_ge(negmax, n + 1)
                nc.scalar.activation(probs[:, u % 2], probs[:, u % 2], ACT.Exp, bias=nmax[:, u % 2:u % 2 + 1], scale=1.0,
                                     accum_out=zsum[:, u:u + 1]).then_inc(exps, 1)

            act.dma_start(wqk_sb[:], wqk[0]).then_inc(wqk_in, 16)
            nc.scalar.preload_act_table_set("natural_log_exp_and_others")
            act.wait_ge(xnT_ps, 1)
            nc.scalar.copy(xnT[:].rearrange("p k t -> p (k t)"), tr_ps[:, 0]).then_inc(xnT_ok, 1)
            act.wait_ge(q_ps, 1)
            nc.scalar.copy(qT[:].rearrange("p h t -> p (h t)"), misc_ps[:]).then_inc(q_ok, 1)
            act.wait_ge(qk_ps, 1)
            nc.scalar.copy(qk_hi[:], misc_ps[:]).then_inc(qkhi_ok, 1)
            iteration(0, False, True)
            with act.Fori(1, NKV - 1) as i:
                iteration(i, True, True)
            iteration(NKV - 1, True, False)
            act.wait_ge(wvo_ps, NKV)
            nc.scalar.copy(wvo_h[:].rearrange("p h d -> p (h d)"), misc_ps[:]).then_inc(wvo_ok, 1)
            high_parts(4 * NKV - 1, 3)
            act.wait_ge(vec_in, 16 * N_VEC)
            nc.scalar.activation(a_rate[:], alog, ACT.Exp).then_inc(ahead_exp, 1)

            act.wait_ge(xnT_ps, 2)
            nc.scalar.copy(x2T[:].rearrange("p k t -> p (k t)"), tr_ps[:, 0]).then_inc(xnT_ok, 1)
            act.wait_ge(dt_abs, 1)
            nc.scalar.activation(dtv[:, 4], dtv[:, 3], ACT.Exp).then_inc(dt_exp, 1)

            def first_tap(order, c):
                act.wait_ge(xbc_ps, order + 1)
                for j in (2 * c, 2 * c + 1):
                    last = nc.scalar.activation(conv[:, j], sc_ps[:, c].rearrange("p (j b t) -> p j b t", j=2, b=B)[:, j % 2],
                                                ACT.Identity, bias=convb[:, j:j + 1], scale=convw[:, j, CW - 1:CW])
                last.then_inc(tap0, 1)

            first_tap(0, 2)
            act.wait_ge(dt_one, 1)
            nc.scalar.activation(dtv[:, 8], dtv[:, 5], ACT.Ln).then_inc(dt_ln, 1)
            first_tap(1, 0)
            first_tap(2, 1)
            act.wait_ge(ends_ps, 1)
            nc.scalar.activation(ends[:].rearrange("p k b h -> p (k b h)"), tr_ps[:, 1, 0:3 * B * NH], ACT.Exp).then_inc(ends_ok, 1)
            for b in range(B):
                act.wait_ge(seg_ps, b + 1)
                nc.scalar.activation(decay[:, b].rearrange("p h t -> p (h t)"), tr_ps[:, b], ACT.Exp).then_inc(decay_ok, 1)
            for order, c in enumerate((2, 0, 1)):
                act.wait_ge(taps, 6 * (order + 1))
                nc.scalar.activation(xc[:, 2 * c:2 * c + 2], conv[:, 2 * c:2 * c + 2], ACT.Silu).then_inc(xc_ok, 1)
            for b in range(B):
                act.wait_ge(z_ps, b + 1)
                nc.scalar.activation(sz[:, b], sc_ps[:, 3] if b == 0 else pv_ps[:], ACT.Silu).then_inc(sz_ok, 1)
            for b in range(B):
                act.wait_ge(y2_ok, b + 1)
                nc.scalar.activation(ysq[:, b], y2[:, b], ACT.Square, accum_out=ss[:, b:b + 1]).then_inc(sq_ok, 1)
                act.wait_ge(yT_ps, b + 1)
                nc.scalar.copy(yT[:, b].rearrange("p j t -> p (j t)"), tr_ps[:, b]).then_inc(yT_ok, 1)

            act.wait_ge(xnT_ps, 3)
            nc.scalar.copy(x3T[:].rearrange("p k t -> p (k t)"), tr_ps[:, 0]).then_inc(xnT_ok, 1)
            act.wait_ge(gate_ps, 1)
            nc.scalar.activation(sg[:].rearrange("p b e -> p (b e)"), pv_ps[:, 0:B * E], ACT.Sigmoid).then_inc(sg_ok, 1)

            def expert_act(m, k, first):
                act.wait_ge(h_ps, m + 1)
                if not first:
                    act.wait_ge(h_ok, m - 3)
                nc.scalar.activation(hs[:, k], sc_ps[:, k, 0:B * P], ACT.Silu).then_inc(h_act, 1)

            for k in range(TPB):
                expert_act(k, k, True)
            act.wait_ge(combT_ps, 1)
            nc.scalar.copy(comb3T[:], misc_ps[0:W3, 0:B * P]).then_inc(combT_ok, 1)
            with act.Fori(1, NM // TPB) as r:
                for k in range(TPB):
                    expert_act(TPB * r + k, k, False)

        @block.vector
        def _(dve):
            def normalise(dst, src, turn):
                for b in range(B):
                    nc.vector.bn_stats(stats[:, b], src[:, b]).then_inc(bn_done, 1)
                for b in range(B):
                    dve.wait_ge(bn_done, B * (turn - 1) + b + 1)
                    nc.vector.bn_aggr(mv[:, b], stats[:, b]).then_inc(mv_ok, 1)
                dve.wait_ge(mv_ok, B * turn)
                nc.vector.tensor_scalar(vare[:], mv[:, :, 1], EPS, None, ALU.add).then_inc(var_ok, 1)
                dve.wait_ge(rstd_ok, turn)
                for b in range(B):
                    nc.vector.tensor_scalar(dst[:, b], src[:, b], mv[:, b, 0:1], rstd[:, b:b + 1],
                                            ALU.subtract, ALU.mult).then_inc(xn_ok, 1)

            def split_context():
                dve.wait_ge(ctxT_in[0], 16)
                nc.vector.tensor_copy(ctxT_hi[0][:], ctxT_raw[0][:]).then_inc(split_T0, 1)
                dve.wait_ge(split_T0, 1)
                nc.vector.tensor_tensor(ctxT_lo[0][:], ctxT_raw[0][:], ctxT_hi[0][:].bitcast(F32),
                                        ALU.subtract).then_inc(split_T0, 1)

            def penalties(b):
                nc.vector.tensor_scalar(pen[:, b], mask_u8[:, b], -1.0, -MASKED, ALU.add, ALU.mult).then_inc(pen_ok, 1)
                dve.wait_ge(pen_ok, b + 1)

            def valid(b):
                nc.vector.tensor_reduce(any_valid[:, b:b + 1], pen[:, b], AX_X, ALU.max).then_inc(any_ok, 1)
                dve.wait_ge(any_ok, 2 * b + 1)
                nc.vector.tensor_scalar(any_valid[:, b:b + 1], any_valid[:, b:b + 1], 0.0, None, ALU.is_ge).then_inc(any_ok, 1)

            def take_outT(p):
                dve.wait_ge(pv, p + 1)
                nc.vector.tensor_reduce(outT[:], pv_ps[:].rearrange("p (z t) -> p t z", z=2), AX_X, ALU.add).then_inc(outT_ok, 1)

            def take_y(p, pp):
                dve.wait_ge(y_ps, p + 1)
                dve.wait_ge(recips, p + 1)
                for h in range(2):
                    dve.wait_ge(y_ok, 2 * p + h + 1)
                    nc.vector.scalar_tensor_tensor(out=yacc[:, pp], in0=misc_ps[:, h * D:(h + 1) * D], scalar=rz[:, pp, h:h + 1],
                                                   in1=yacc[:, pp], op0=ALU.mult, op1=ALU.add).then_inc(y_ok, 1)

            def low_part(m, mu, g):
                dve.wait_ge(turned_hi, 4 * m + (g + 1))
                c = (mu % 2) * P
                t4 = slice(4 * g, 4 * g + 4)
                nc.vector.tensor_tensor(pt[mu // 2][:, t4, 2 * P + c:3 * P + c], tr_ps[:, g % 2].rearrange("p (s t) -> p s t", s=4),
                                        pt[mu // 2][:, t4, c:c + P].bitcast(F32), ALU.subtract).then_inc(turned_lo, 1)

            def low_q(turn):
                dve.wait_ge(qkhi_ok, turn)
                nc.vector.tensor_tensor(qk_lo[:], misc_ps[:], qk_hi[:].bitcast(F32), ALU.subtract).then_inc(qk_ok, 1)

            def recip(p, pp, units):
                dve.wait_ge(exps, units)
                nc.vector.reciprocal(rz[:, pp], zsum[:, 2 * pp:2 * pp + 2]).then_inc(recips, 1)

            def iteration(i, prev, more):
                for u in range(4):
                    n, b = 4 * i + u, u // 2
                    if u == 1 and prev:
                        take_outT(2 * i - 2)
                    if u == 3 and prev:
                        take_outT(2 * i - 1)
                    for j in range(NB):
                        dve.wait_ge(scores, 4 * n + (j + 1))
                        nc.vector.memset(taker[:, j:j + 1], 0.0)
                        js = slice(j * BANK, (j + 1) * BANK)
                        nc.vector.tensor_tensor_reduce(probs[:, u % 2, js], sc_ps[:, j], pen[:, b, js], SCALE, -3e38,
                                                       ALU.add, ALU.max, mx[:, u % 2, j:j + 1]).then_inc(masked, 1)
                    dve.wait_ge(masked, 4 * n + 4)
                    nc.vector.tensor_reduce(nmax[:, u % 2:u % 2 + 1], mx[:, u % 2], AX_X, ALU.max, negate=True).then_inc(negmax, 1)
                    if u == 3 and more:
                        low_q(i + 2)
                    for g in range(4):
                        if prev or u > 0:
                            low_part(n - 1, (u + 3) % 4, g)
                        if g == 0 and u == 1 and prev:
                            take_y(2 * i - 2, 0)
                        if g == 2 and u == 3 and prev:
                            take_y(2 * i - 1, 1)
                    if u == 0 and prev:
                        recip(2 * i - 1, 1, 4 * i)
                    if u == 2:
                        recip(2 * i, 0, 4 * i + 2)

            nc.vector.memset(yacc[:], 0.0).then_inc(y_ok, 1)
            dve.wait_ge(x_in, 16)
            normalise(xn, x_sb, 1)
            split_context()
            dve.wait_ge(mask_in, 16)
            penalties(0)
            low_q(1)
            penalties(1)
            iteration(0, False, True)
            with dve.Fori(1, NKV - 1) as i:
                iteration(i, True, True)
            iteration(NKV - 1, True, False)
            for g in range(4):
                low_part(4 * NKV - 1, 3, g)
            recip(2 * NKV - 1, 1, 4 * NKV)
            take_outT(2 * NKV - 2)
            take_y(2 * NKV - 2, 0)
            for b in range(B):
                valid(b)
            take_outT(2 * NKV - 1)
            take_y(2 * NKV - 1, 1)
            dve.wait_ge(any_ok, 2 * B)
            dve.wait_ge(y_ok, 4 * NKV + 1)
            for b in range(B):
                nc.vector.scalar_tensor_tensor(out=x1[:, b], in0=yacc[:, b], scalar=any_valid[:, b:b + 1], in1=x_sb[:, b],
                                               op0=ALU.mult, op1=ALU.add).then_inc(x1_ok, 1)
            dve.wait_ge(x1_ok, B)

            done = [0]

            def link(ins):
                done[0] += 1
                ins.then_inc(dve_step, 1)
                dve.wait_ge(dve_step, done[0])

            normalise(xn2, x1, 2)
            v, pos, neg, nab, e, u1, um, one, lnu, num, den, rec, q1, q2 = (dtv[:, k] for k in range(14))
            dve.wait_ge(dt_ps, 1)
            dve.wait_ge(vec_in, 16 * N_VEC)
            link(nc.vector.tensor_tensor(v, misc_ps[:, 0:B * NH].rearrange("p (b h) -> p b h", b=B),
                                         dtb.unsqueeze(1).broadcast_to([P, B, NH]), ALU.add))
            nc.vector.tensor_scalar(pos, v, 0.0, None, ALU.max)
            link(nc.vector.tensor_scalar(neg, v, 0.0, None, ALU.min))
            nc.vector.tensor_tensor(nab, neg, pos, ALU.subtract).then_inc(dt_abs, 1)

            def other_taps(order, c):
                dve.wait_ge(tap0, order + 1)
                for n in range(6):
                    j, k = 2 * c + n % 2, n // 2 + 1
                    if n >= 2:
                        dve.wait_ge(taps, 6 * order + n - 1)
                    nc.vector.scalar_tensor_tensor(
                        out=conv[:, j, :, k:], in0=sc_ps[:, c].rearrange("p (j b t) -> p j b t", j=2, b=B)[:, j % 2, :, 0:P - k],
                        scalar=convw[:, j, CW - 1 - k:CW - k], in1=conv[:, j, :, k:], op0=ALU.mult, op1=ALU.add).then_inc(taps, 1)

            other_taps(0, 2)
            dve.wait_ge(dt_exp, 1)
            link(nc.vector.tensor_scalar(u1, e, 1.0, None, ALU.add))
            nc.vector.tensor_scalar(um, u1, -1.0, None, ALU.add).then_inc(dt_one, 1)
            dve.wait_ge(dt_one, 1)
            link(nc.vector.tensor_scalar(one, um, 0.0, None, ALU.is_equal))
            link(nc.vector.tensor_tensor(den, um, one, ALU.add))
            link(nc.vector.reciprocal(rec, den))
            link(nc.vector.tensor_tensor(q1, rec, e, ALU.mult))
            dve.wait_ge(dt_ln, 1)
            link(nc.vector.tensor_tensor(num, lnu, one, ALU.add))
            link(nc.vector.tensor_tensor(q2, num, q1, ALU.mult))
            link(nc.vector.tensor_tensor(dt[:], pos, q2, ALU.add))
            dve.wait_ge(ahead_exp, 1)
            nc.vector.scalar_tensor_tensor(out=a_dt[:], in0=dt[:], scalar=-1.0, in1=a_rate[:].unsqueeze(1).broadcast_to([P, B, NH]),
                                           op0=ALU.mult, op1=ALU.mult).then_inc(a_ok, 1)
            dve.wait_ge(a_ok, 1)
            dve.wait_ge(const_ok, 8)
            nc.vector.tensor_tensor(steps[:, 0], a_dt[:, 0].unsqueeze(2).broadcast_to([P, NH, C]),
                                    upto_c[:].unsqueeze(1).broadcast_to([P, NH, C]), ALU.mult).then_inc(steps0_ok, 1)
            other_taps(1, 0)
            other_taps(2, 1)
            dve.wait_ge(g_ps, 1)
            nc.vector.tensor_copy(bc[:].rearrange("p b t -> p (b t)"), misc_ps[:, 0:B * P]).then_inc(bc_ok, 1)
            dve.wait_ge(bc_ok, 1)
            nc.vector.tensor_tensor(bc_in[:], bc[:], upto[:].unsqueeze(1).broadcast_to([P, B, P]), ALU.mult).then_inc(bcin_ok, 1)
            for b in range(B):
                dve.wait_ge(xh_ps, b + 1)
                heads = sc_ps[:, b].rearrange("p (h d) -> p h d", h=NH)
                nc.vector.tensor_tensor(xdt[:, b], heads, dt[:, b].unsqueeze(2).broadcast_to([P, NH, HD]), ALU.mult).then_inc(xdt_ok, 1)
                link(nc.vector.tensor_tensor(xd[:, b], heads, dskip.unsqueeze(2).broadcast_to([P, NH, HD]), ALU.mult))
                dve.wait_ge(bcin_ok, 1)
                dve.wait_ge(decay_ok, b + 1)
                nc.vector.tensor_tensor(mT[:, b].rearrange("p h (c t) -> p h c t", c=2),
                                        decay[:, b].unsqueeze(2).broadcast_to([P, NH, 2, C]),
                                        bc_in[:, b].rearrange("p (c t) -> p c t", c=2).unsqueeze(1).broadcast_to([P, NH, 2, C]),
                                        ALU.mult).then_inc(mT_ok, 1)
            for b in range(B):
                dve.wait_ge(off_ps, b + 1)
                dve.wait_ge(ends_ok, 1)
                link(nc.vector.tensor_tensor(y_off[:, b], (sc_ps[:, 3] if b == 0 else pv_ps[:]).rearrange("p (h d) -> p h d", h=NH),
                                             ends[:, 2, b].unsqueeze(2).broadcast_to([P, NH, HD]), ALU.mult))
                link(nc.vector.tensor_tensor(y_add[:, b], y_off[:, b], xd[:, b], ALU.add))
                dve.wait_ge(ssm_ps, b + 1)
                link(nc.vector.tensor_tensor(y1[:, b], sc_ps[:, 2] if b == 0 else misc_ps[:], y_add[:, b].rearrange("p h d -> p (h d)"), ALU.add))
                dve.wait_ge(sz_ok, b + 1)
                nc.vector.tensor_tensor(y2[:, b], y1[:, b], sz[:, b], ALU.mult).then_inc(y2_ok, 1)
            dve.wait_ge(sq_ok, B)
            nc.vector.tensor_scalar(sse[:], ss[:], 1.0 / DI, EPS, ALU.mult, ALU.add).then_inc(ss_ok, 1)
            dve.wait_ge(rinv_ok, 1)
            for b in range(B):
                dve.wait_ge(o_ps, b + 1)
                nc.vector.scalar_tensor_tensor(out=x2[:, b], in0=sc_ps[:, b, 0:D], scalar=rinv[:, b:b + 1],
                                               in1=x1[:, b], op0=ALU.mult, op1=ALU.add).then_inc(x2_ok, 1)
            dve.wait_ge(x2_ok, B)

            normalise(xn3, x2, 3)
            dve.wait_ge(sg_ok, 1)
            sg4 = sg[:].rearrange("p b (g k) -> p (b g) k", k=E // G)
            nc.vector.tensor_tensor(pairs[:, :, 0:3], sg4[:, :, 0:3], sg4[:, :, 1:4], ALU.add)
            nc.vector.tensor_tensor(pairs[:, :, 3:5], sg4[:, :, 0:2], sg4[:, :, 2:4], ALU.add)
            link(nc.vector.tensor_tensor(pairs[:, :, 5:6], sg4[:, :, 0:1], sg4[:, :, 3:4], ALU.add))
            link(nc.vector.tensor_reduce(gsum[:].rearrange("p b g -> p (b g)"), pairs[:], AX_X, ALU.max))

            def two_best(val, n, low, cmp, rank, sel):
                mine = val[:].unsqueeze(3).broadcast_to([P, B, n, n])
                theirs = val[:].unsqueeze(2).broadcast_to([P, B, n, n])
                link(nc.vector.tensor_tensor(cmp[:, 0], theirs, mine, ALU.is_equal))
                for b in range(B):
                    last = nc.vector.tensor_tensor(cmp[:, 1, b], cmp[:, 0, b], low[:], ALU.mult)
                link(last)
                link(nc.vector.tensor_tensor(cmp[:, 2], theirs, mine, ALU.is_gt))
                link(nc.vector.tensor_tensor(cmp[:, 0], cmp[:, 2], cmp[:, 1], ALU.add))
                link(nc.vector.tensor_reduce(rank[:], cmp[:, 0], AX_X, ALU.add))
                link(nc.vector.tensor_scalar(sel[:], rank[:], 1.5, None, ALU.is_lt))

            dve.wait_ge(order_ok, 3)
            two_best(gsum, G, low_g, cmp_g, rank_g, sel_g)
            link(nc.vector.tensor_tensor(cand[:].rearrange("p b (g k) -> p (b g) k", k=E // G), sg4,
                                         sel_g[:].rearrange("p b g -> p (b g)").unsqueeze(2).broadcast_to([P, B * G, E // G]), ALU.mult))
            two_best(cand, E, low_e, cmp_e, rank_e, sel_e)
            link(nc.vector.tensor_tensor(wsel[:], cand[:], sel_e[:], ALU.mult))
            link(nc.vector.tensor_reduce(wsum[:], wsel[:], AX_X, ALU.add))
            link(nc.vector.tensor_scalar(wsum[:], wsum[:], 1e-20, None, ALU.add))
            link(nc.vector.reciprocal(wrec[:], wsum[:]))
            link(nc.vector.tensor_tensor(comb[:], wsel[:], wrec[:].unsqueeze(2).broadcast_to([P, B, E]), ALU.mult))
            link(nc.vector.tensor_copy(comb_hi[:], comb[:]))
            nc.vector.tensor_copy(comb3[:, :, 0:E], comb_hi[:])
            link(nc.vector.tensor_tensor(comb_rest[:], comb[:], comb_hi[:], ALU.subtract))
            link(nc.vector.tensor_copy(comb_mid[:], comb_rest[:]))
            nc.vector.tensor_copy(comb3[:, :, PART:PART + E], comb_mid[:])
            nc.vector.tensor_tensor(comb3[:, :, 2 * PART:2 * PART + E], comb_rest[:], comb_mid[:], ALU.subtract).then_inc(comb_ok, 1)

            def expert_weigh(m, k, first):
                dve.wait_ge(c_ps, m + 1)
                dve.wait_ge(h_act, m + 1)
                if not first:
                    dve.wait_ge(h_used, m - 3)
                nc.vector.tensor_tensor(hc[:, k], tr_ps[:, k % 2, 0:B * P], hs[:, k], ALU.mult).then_inc(h_ok, 1)

            for k in range(TPB):
                expert_weigh(k, k, True)
            with dve.Fori(1, NM // TPB) as r:
                for k in range(TPB):
                    expert_weigh(TPB * r + k, k, False)
            dve.wait_ge(h_used, NM)
            for b in range(B):
                nc.vector.tensor_tensor(res[:, b], (pv_ps if b == 0 else misc_ps)[:, 0:D], x2[:, b], ALU.add).then_inc(res_ok, 1)


def kernel(x, ctx_1024, mask_BxS2_bf1, L0_xattn_Wq, L0_xattn_Wk, L0_xattn_Wv, L0_xattn_Wo, L0_attn_in_proj_w,
           L0_attn_conv_w, L0_attn_conv_b, L0_attn_A_log, L0_attn_D, L0_attn_dt_bias, L0_attn_norm_w,
           L0_attn_out_proj_w, L0_ffn_gate_w, L0_ffn_w1, L0_ffn_w2, L0_ffn_sw1, L0_ffn_sw2):
    import numpy as np
    import concourse.bacc as bacc
    from concourse.bass_utils import run_bass_kernel_spmd

    def flat(a):
        return np.ascontiguousarray(np.asarray(a))

    ctx = flat(ctx_1024)
    wq = flat(L0_xattn_Wq).reshape(KT, P, NKV, 2 * P).transpose(2, 1, 0, 3).reshape(NKV, P, KT * 2 * P)
    wk_t = flat(L0_xattn_Wk).reshape(P, NKV, P).transpose(1, 2, 0)
    wv_t = flat(L0_xattn_Wv).reshape(P, NKV, P).transpose(1, 2, 0)
    wo = flat(L0_xattn_Wo).reshape(NKV, 2, P, D).transpose(0, 2, 1, 3).reshape(NKV, P, 2 * D)
    w1 = np.concatenate([flat(L0_ffn_w1), flat(L0_ffn_sw1)]).transpose(1, 0, 2).reshape(D, (E + 1) * H)
    w1 = np.pad(w1, ((0, 0), (0, NM * P - (E + 1) * H))).reshape(KT, P, NM, P).transpose(2, 1, 0, 3)
    w2 = np.concatenate([flat(L0_ffn_w2), flat(L0_ffn_sw2)]).reshape((E + 1) * H, D)
    w2 = np.pad(w2, ((0, NM * P - (E + 1) * H), (0, 0))).reshape(NM, P, D)
    expert_rows = np.zeros((W3, NM * P), np.uint16)
    for part in range(3):
        for e in range(E + 1):
            expert_rows[part * PART + e, e * H:(e + 1) * H] = 0x3F80

    small_by_row = np.concatenate([
        flat(L0_attn_conv_w).reshape(NX, P, CW).transpose(1, 0, 2).reshape(P, NX * CW), flat(L0_attn_conv_b).reshape(NX, P).T,
        flat(L0_attn_norm_w).reshape(DI // P, P).T, flat(L0_ffn_gate_w).T.reshape(KT, P, E).transpose(1, 0, 2).reshape(P, KT * E),
    ], axis=1)
    small_by_head = np.concatenate([flat(L0_attn_A_log), flat(L0_attn_D), flat(L0_attn_dt_bias)])

    arrays = {
        "x": flat(x), "ctx": ctx, "ctx_t": ctx.transpose(0, 2, 1), "mask": flat(mask_BxS2_bf1).view(np.uint8),
        "wqk": np.concatenate([wq, wk_t], axis=2), "wvo": np.concatenate([wv_t, wo], axis=2),
        "win_t": flat(L0_attn_in_proj_w).T, "small_by_row": small_by_row, "small_by_head": small_by_head,
        "wout_t": flat(L0_attn_out_proj_w).T,
        "w1": w1, "w2": w2, "expert_rows": expert_rows,
    }
    nc = bacc.Bacc("TRN2", target_bir_lowering=False, num_devices=1)
    arrays = {f"in_{name}": np.ascontiguousarray(a) for name, a in arrays.items()}
    args = [nc.dram_tensor(name, a.shape, mybir.dt.from_np(a.dtype), kind="ExternalInput").ap() for name, a in arrays.items()]
    out = nc.dram_tensor("out", (B, P, D), F32, kind="ExternalOutput").ap()
    cross_attention_ssm_moe(nc, *args, out)
    return run_bass_kernel_spmd(nc, [arrays], core_ids=[0]).results[0]["out"]
```

```python
from contextlib import ExitStack

import concourse.bass as bass
from concourse import mybir

ALU = mybir.AluOpType
ACT = mybir.ActivationFunctionType
AX_X = mybir.AxisListType.X
F32 = mybir.dt.float32
F32R = mybir.dt.float32r
BF16 = mybir.dt.bfloat16
U8 = mybir.dt.uint8

P = 128
B = 2
D = 256
KT = D // P
S = 2048
ST = S // P
BANK = 512
NB = S // BANK
NKV = 8
SCALE = float(P) ** -0.5
MASKED = -1e30

DI = 512
NH = 8
HD = DI // NH
C = P // 2
NX = 6
NI = 2 * DI + 2 * P + NH
CW = 4

WARM_START, WARM_OUT, WARM_TURN, WARM_SSM, WARM_CONV, WARM_EXPERTS, WARM_PACKS, WARM_GATE = 20, 18, 7, 36, 10, 30, 12, 8

E = 16
H = 176
NM = 24
G = 4
TPB = 4
LAG = 2
NPK = NM + LAG
PART = 32
W3 = 3 * PART
N_VEC = 2
EPS = 1e-5


def cross_attention_ssm_moe(nc, x, ctx, ctx_t, mask, wqk, wvo, win_t, small_by_row, small_by_head, wout_t, w_packs,
                            expert_rows, out):
    with ExitStack() as stack:
        def sem(name):
            return stack.enter_context(nc.semaphore(name))

        def psum(name, shape):
            return stack.enter_context(nc.psum_tensor(name, shape, F32))

        def sbuf_in(scope):
            return lambda name, shape, dt=F32: scope.enter_context(nc.sbuf_tensor(name, shape, dt))

        sc_ps = psum("sc_ps", [P, NB, BANK])
        tr_ps = psum("tr_ps", [P, 2, BANK])
        pv_ps = psum("pv_ps", [P, BANK])
        misc_ps = psum("misc_ps", [P, BANK])

        keep = sbuf_in(stack)
        x_sb = keep("x_sb", [P, B, D])
        ident = keep("ident", [P, P])
        after = keep("after", [P, P])
        after_in = keep("after_in", [P, P])
        upto = keep("upto", [P, P])
        upto_c = keep("upto_c", [P, C])
        win = keep("win", [P, KT, NI])
        by_row = keep("by_row", [P, NX * CW + NX + 2 * (DI // P) + KT * E + E])
        by_head = keep("by_head", [P, 2, NH])
        a_rate = keep("a_rate", [P, NH])
        any_valid = keep("any_valid", [P, B])
        stats = keep("stats", [P, B, 6])
        mv = keep("mv", [P, B, 2])
        vare = keep("vare", [P, B])
        rstd = keep("rstd", [P, B])
        zero = keep("zero", [P, 1])
        mhalf = keep("mhalf", [P, B])

        attn = ExitStack()
        with ExitStack() as staging:
            ctxT_raw = [sbuf_in(staging)(f"ctxT_raw{b}", [P, S]) for b in range(B)]
            ctx_raw = [sbuf_in(staging)(f"ctx_raw{b}", [P, ST, P]) for b in range(B)]
            mask_u8 = sbuf_in(staging)("mask_u8", [P, B, S], U8)
            xn = sbuf_in(staging)("xn", [P, B, D])
        a_sb = sbuf_in(attn)
        pt = [None, None]
        pt[1] = a_sb("pt1", [P, ST, BANK], F32R)
        pt[0] = a_sb("pt0", [P, ST, BANK], F32R)
        ctxT_hi = [a_sb(f"ctxT_hi{b}", [P, S], F32R) for b in range(B)]
        ctxT_lo = [a_sb(f"ctxT_lo{b}", [P, S], F32R) for b in range(B)]
        ctx_hi = [a_sb(f"ctx_hi{b}", [P, ST, P], F32R) for b in range(B)]
        ctx_lo = [a_sb(f"ctx_lo{b}", [P, ST, P], F32R) for b in range(B)]
        probs = a_sb("probs", [P, 2, S])
        pen = a_sb("pen", [P, B, S], BF16)
        wqk_sb = a_sb("wqk_sb", [P, KT * 2 * P + P])
        wvo_sb = a_sb("wvo_sb", [P, P + 2 * D])
        wqk_hi = a_sb("wqk_hi", [P, KT * 2 * P + P], F32R)
        wqk_lo = a_sb("wqk_lo", [P, KT * 2 * P + P], F32R)
        wvo_hi = a_sb("wvo_hi", [P, P + 2 * D], F32R)
        wvo_lo = a_sb("wvo_lo", [P, P + 2 * D], F32R)
        xnT_hi = a_sb("xnT_hi", [P, KT * B * P], F32R)
        xnT_lo = a_sb("xnT_lo", [P, KT * B * P], F32R)
        qT_hi = a_sb("qT_hi", [P, 2 * B * P], F32R)
        qT_lo = a_sb("qT_lo", [P, 2 * B * P], F32R)
        qk_hi = a_sb("qk_hi", [P, 2 * B * P], F32R)
        qk_lo = a_sb("qk_lo", [P, 2 * B * P], F32R)
        fold_raw = a_sb("fold_raw", [P, 2 * D])
        y_new = a_sb("y_new", [P, 2, D])
        fold_hi = a_sb("fold_hi", [P, 2 * D], F32R)
        fold_lo = a_sb("fold_lo", [P, 2 * D], F32R)
        outT = a_sb("outT", [P, 2 * P])
        outT_hi = a_sb("outT_hi", [P, 2 * P], F32R)
        outT_lo = a_sb("outT_lo", [P, 2 * P], F32R)
        yacc = a_sb("yacc", [P, B, D])
        mx = a_sb("mx", [P, 2, NB])
        taker = a_sb("taker", [P, NB])
        nmax = a_sb("nmax", [P, 2])
        zsum = a_sb("zsum", [P, 4])
        rz = a_sb("rz", [P, 2, 2])
        attn.close()

        late = ExitStack()
        l_sb = sbuf_in(late)
        x1 = l_sb("x1", [P, B, D])
        xn2 = l_sb("xn2", [P, B, D])
        x2T = l_sb("x2T", [P, KT, B * P])
        wout = l_sb("wout", [P, DI // P, D])
        conv = l_sb("conv", [P, NX, B, P])
        xc = l_sb("xc", [P, NX, B, P])
        dtv = l_sb("dtv", [P, 14, B, NH])
        dt = l_sb("dt", [P, B, NH])
        a_dt = l_sb("a_dt", [P, B, NH])
        ends = l_sb("ends", [P, 3, B, NH])
        steps = l_sb("steps", [P, B, NH, C])
        decay = l_sb("decay", [P, B, NH, C])
        bc = l_sb("bc", [P, B, P])
        bc_in = l_sb("bc_in", [P, B, P])
        mT = l_sb("mT", [P, B, NH, P])
        xdt = l_sb("xdt", [P, B, NH, HD])
        skip = l_sb("skip", [P, DI // P, P])
        xq = l_sb("xq", [P, B, 2, NH, HD])
        y_off = l_sb("y_off", [P, B, NH, HD])
        sz = l_sb("sz", [P, B, DI])
        y1 = l_sb("y1", [P, B, DI])
        y2 = l_sb("y2", [P, B, DI])
        ysq = l_sb("ysq", [P, B, DI])
        ss = l_sb("ss", [P, B])
        sse = l_sb("sse", [P, B])
        rinv = l_sb("rinv", [P, B])
        yT = l_sb("yT", [P, B, DI // P, P])
        x2 = l_sb("x2", [P, B, D])
        xn3 = l_sb("xn3", [P, B, D])
        x3T = l_sb("x3T", [P, KT, B * P])
        x3T_hi = l_sb("x3T_hi", [P, KT, B * P], F32R)
        x3T_lo = l_sb("x3T_lo", [P, KT, B * P], F32R)
        packs = l_sb("packs", [P, TPB, KT * P + D])
        packs_hi = l_sb("packs_hi", [P, TPB, KT * P + D], F32R)
        packs_lo = l_sb("packs_lo", [P, TPB, KT * P + D], F32R)
        sg = l_sb("sg", [P, B, E])
        pairs = l_sb("pairs", [P, B * G, 6])
        gsum = l_sb("gsum", [P, B, G])
        low_g = l_sb("low_g", [P, G, G])
        cmp_g = l_sb("cmp_g", [P, 3, B, G, G])
        rank_g = l_sb("rank_g", [P, B, G])
        sel_g = l_sb("sel_g", [P, B, G])
        cand = l_sb("cand", [P, B, E])
        best = l_sb("best", [P, 2, B])
        ties = l_sb("ties", [P, 2, B, E])
        placed = l_sb("placed", [P, 2, B, E])
        place = l_sb("place", [P, 2, B])
        picked = l_sb("picked", [P, 2, B, E])
        others = l_sb("others", [P, B, E])
        sel_e = l_sb("sel_e", [P, B, E])
        wsel = l_sb("wsel", [P, B, E])
        wsum = l_sb("wsum", [P, B])
        wrec = l_sb("wrec", [P, B])
        comb = l_sb("comb", [P, B, E])
        comb_hi = l_sb("comb_hi", [P, B, E], BF16)
        comb_rest = l_sb("comb_rest", [P, B, E])
        comb_mid = l_sb("comb_mid", [P, B, E], BF16)
        comb3 = l_sb("comb3", [P, B, W3])
        comb3T = l_sb("comb3T", [W3, B * P], BF16)
        rows = l_sb("rows", [W3, NM * P], BF16)
        hs = l_sb("hs", [P, 4, B * P])
        hc = l_sb("hc", [P, 4, B * P])
        hc_hi = l_sb("hc_hi", [P, 4, B * P], F32R)
        hc_lo = l_sb("hc_lo", [P, 4, B * P], F32R)
        res = l_sb("res", [P, B, D])
        late.close()

        cut = [0]
        for width in (NX * CW, NX, DI // P, DI // P, KT * E, E):
            cut.append(cut[-1] + width)
        convw = by_row[:, cut[0]:cut[1]].rearrange("p (j w) -> p j w", w=CW)
        convb, normw = by_row[:, cut[1]:cut[2]], by_row[:, cut[2]:cut[3]]
        dskip, places = by_row[:, cut[3]:cut[4]], by_row[:, cut[5]:cut[6]]
        gate = by_row[:, cut[4]:cut[5]].rearrange("p (k e) -> p k e", e=E)
        alog, dtb = (by_head[:, k] for k in range(2))

        x_in, mask_in, vec_in, rows_in = sem("x_in"), sem("mask_in"), sem("vec_in"), sem("rows_in")
        ctxT_in = [sem(f"ctxT_in{b}") for b in range(B)]
        ctx_in = [sem(f"ctx_in{b}") for b in range(B)]
        wqk_in, wvo_in, win_in, wout_in = sem("wqk_in"), sem("wvo_in"), sem("win_in"), sem("wout_in")
        packs_in = [sem(f"packs_in{k}") for k in range(TPB)]
        out_sent = sem("out_sent")

        const_set, const_ok, split_hi, split_lo = sem("const_set"), sem("const_ok"), sem("split_hi"), sem("split_lo")
        split_T0, pen_ok, any_ok, wout_ok = sem("split_T0"), sem("pen_ok"), sem("any_ok"), sem("wout_ok")
        ahead_exp = sem("ahead_exp")
        bn_done, mv_ok, var_ok, rstd_ok = sem("bn_done"), sem("mv_ok"), sem("var_ok"), sem("rstd_ok")
        xn_ok, xnT_ps, xnThi_ok, xnT_ok = sem("xn_ok"), sem("xnT_ps"), sem("xnThi_ok"), sem("xnT_ok")
        scores, masked, negmax, exps = sem("scores"), sem("masked"), sem("negmax"), sem("exps")
        turned, turned_hi, turned_lo = sem("turned"), sem("turned_hi"), sem("turned_lo")
        pv, pv_read, outThi_ok, outT_ok = sem("pv"), sem("pv_read"), sem("outThi_ok"), sem("outT_ok")
        wqk_high, wqk_split, wvo_high, wvo_split = sem("wqk_high"), sem("wqk_split"), sem("wvo_high"), sem("wvo_split")
        qhi_ok, foldhi_ok, foldraw_ok, y_read = sem("qhi_ok"), sem("foldhi_ok"), sem("foldraw_ok"), sem("y_read")
        q_ps, q_ok, qk_ps, qkhi_ok, qk_ok = sem("q_ps"), sem("q_ok"), sem("qk_ps"), sem("qkhi_ok"), sem("qk_ok")
        fold_ps, fold_ok, y_ps, y_ok, recips = sem("fold_ps"), sem("fold_ok"), sem("y_ps"), sem("y_ok"), sem("recips")
        x1_ok = sem("x1_ok")
        dt_ps, dt_abs, dt_exp, dt_one, dt_ln, a_ok = sem("dt_ps"), sem("dt_abs"), sem("dt_exp"), sem("dt_one"), sem("dt_ln"), sem("a_ok")
        xbc_ps, tap0, taps, xc_ok, z_ps, sz_ok = sem("xbc_ps"), sem("tap0"), sem("taps"), sem("xc_ok"), sem("z_ps"), sem("sz_ok")
        steps0_ok, steps1_ok, seg_ps, decay_ok = sem("steps0_ok"), sem("steps1_ok"), sem("seg_ps"), sem("decay_ok")
        ends_ps, ends_ok, xq_ok, off_ps = sem("ends_ps"), sem("ends_ok"), sem("xq_ok"), sem("off_ps")
        g_ps, bc_ok, bcin_ok, xh_ps, xdt_ok, mT_ok = sem("g_ps"), sem("bc_ok"), sem("bcin_ok"), sem("xh_ps"), sem("xdt_ok"), sem("mT_ok")
        ssm_ps, y2_ok, sq_ok, ss_ok, rinv_ok = sem("ssm_ps"), sem("y2_ok"), sem("sq_ok"), sem("ss_ok"), sem("rinv_ok")
        yT_ps, yT_ok, o_ps, x2_ok = sem("yT_ps"), sem("yT_ok"), sem("o_ps"), sem("x2_ok")
        dve_step = sem("dve_step")
        skip_ok = sem("skip_ok")
        order_set, order_ok = sem("order_set"), sem("order_ok")
        gate_ps, sg_ok, comb_ok, combT_ps, combT_ok = sem("gate_ps"), sem("sg_ok"), sem("comb_ok"), sem("combT_ps"), sem("combT_ok")
        x3hi_ok, x3_ok, packhi_ok, pack_ok = sem("x3hi_ok"), sem("x3_ok"), sem("packhi_ok"), sem("pack_ok")
        h_ps, c_ps, h_act, hc_ok, hchi_ok, h_ok = sem("h_ps"), sem("c_ps"), sem("h_act"), sem("hc_ok"), sem("hchi_ok"), sem("h_ok")
        h_used, first_whole, res_ok = sem("h_used"), sem("first_whole"), sem("res_ok")

        block = stack.enter_context(nc.Block())

        @block.sync
        def _(sp):
            sp.dma_start(x_sb[:], x.rearrange("b t d -> t b d")).then_inc(x_in, 16)
            sp.dma_start(ctxT_raw[0][:], ctx_t[0]).then_inc(ctxT_in[0], 16)
            sp.dma_start(mask_u8[:], mask.partition_broadcast(P)).then_inc(mask_in, 16)
            sp.dma_start(ctxT_raw[1][:], ctx_t[1]).then_inc(ctxT_in[1], 16)
            for b in range(B):
                sp.dma_start(ctx_raw[b][:], ctx[b].rearrange("(n p) v -> p n v", p=P)).then_inc(ctx_in[b], 16)
            sp.dma_start(wvo_sb[:], wvo[0]).then_inc(wvo_in, 16)
            sp.dma_start(by_row[:], small_by_row).then_inc(vec_in, 16)
            sp.dma_start(by_head[:].rearrange("p k h -> p (k h)"), small_by_head.partition_broadcast(P)).then_inc(vec_in, 16)
            sp.wait_ge(wqk_split, 1)
            sp.dma_start(wqk_sb[:], wqk[1]).then_inc(wqk_in, 16)
            sp.dma_start(win[:], win_t.rearrange("(k p) n -> p k n", p=P)).then_inc(win_in, 16)
            with sp.Fori(1, NKV - 1) as i:
                sp.wait_ge(wvo_split, i)
                sp.dma_start(wvo_sb[:], wvo[i]).then_inc(wvo_in, 16)
                sp.wait_ge(wqk_split, i + 1)
                sp.dma_start(wqk_sb[:], wqk[i + 1]).then_inc(wqk_in, 16)
            sp.wait_ge(wvo_split, NKV - 1)
            sp.dma_start(wvo_sb[:], wvo[NKV - 1]).then_inc(wvo_in, 16)
            sp.wait_ge(x1_ok, B)
            sp.dma_start(wout[:], wout_t.rearrange("(j p) n -> p j n", p=P)).then_inc(wout_in, 16)
            sp.dma_start(rows[:], expert_rows.bitcast(BF16)).then_inc(rows_in, 16)

            for k in range(TPB):
                sp.dma_start(packs[:, k], w_packs[k]).then_inc(packs_in[k], 16)

            def refill(r, k):
                sp.wait_ge(pack_ok, TPB * r + (k + 1 - TPB))
                sp.dma_start(packs[:, k], w_packs[TPB * r + k]).then_inc(packs_in[k], 16)

            with sp.Fori(1, NM // TPB) as r:
                for k in range(TPB):
                    refill(r, k)
            for k in range(LAG):
                refill(NM // TPB, k)
            for b in range(B):
                sp.wait_ge(res_ok, b + 1)
                sp.dma_start(out[b], res[:, b]).then_inc(out_sent, 16)
            sp.wait_ge(out_sent, 16 * B)

        @block.gpsimd
        def _(pool):
            pool.memset(ident[:], 1.0).then_inc(const_set, 1)
            pool.memset(mhalf[:], -0.5).then_inc(const_set, 1)
            pool.memset(zero[:], 0.0).then_inc(const_set, 1)
            for tri in (after, after_in, upto):
                pool.memset(tri[:], 1.0).then_inc(const_set, 1)
            pool.memset(upto_c[:], 1.0).then_inc(const_set, 1)
            pool.wait_ge(const_set, 7)
            pool.affine_select(out=ident[:], in_=ident[:], compare_op=ALU.is_equal, fill=0.0, base=0,
                               pattern=[[-1, P]], channel_multiplier=1).then_inc(const_ok, 1)
            pool.wait_ge(var_ok, 1)
            pool.tensor_tensor(rstd[:], vare[:], mhalf[:], ALU.pow).then_inc(rstd_ok, 1)

            def split_wqk(i):
                pool.wait_ge(wqk_in, 16 * i + 16)
                pool.wait_ge(qk_ps, i)
                pool.tensor_tensor(wqk_hi[:], wqk_sb[:], zero[:].broadcast_to(list(wqk_sb.shape)), ALU.add).then_inc(wqk_high, 1)
                pool.wait_ge(wqk_high, i + 1)
                pool.tensor_tensor(wqk_lo[:], wqk_sb[:], wqk_hi[:].bitcast(F32), ALU.subtract).then_inc(wqk_split, 1)

            def split_wvo(i, first):
                pool.wait_ge(wvo_in, 16 * i + 16)
                if not first:
                    pool.wait_ge(fold_ps, i)
                pool.tensor_tensor(wvo_hi[:], wvo_sb[:], zero[:].broadcast_to(list(wvo_sb.shape)), ALU.add).then_inc(wvo_high, 1)
                pool.wait_ge(wvo_high, i + 1)
                pool.tensor_tensor(wvo_lo[:], wvo_sb[:], wvo_hi[:].bitcast(F32), ALU.subtract).then_inc(wvo_split, 1)

            pool.wait_ge(split_hi, 1)
            pool.tensor_tensor(ctxT_lo[1][:], ctxT_raw[1][:], ctxT_hi[1][:].bitcast(F32), ALU.subtract).then_inc(split_lo, 1)
            split_wqk(1)
            for b in range(B):
                pool.wait_ge(split_hi, 2 + 2 * b)
                pool.tensor_tensor(ctx_lo[b][:], ctx_raw[b][:], ctx_hi[b][:].bitcast(F32), ALU.subtract).then_inc(split_lo, 1)
            split_wvo(0, True)
            for tri in (after, after_in):
                pool.affine_select(out=tri[:], in_=tri[:], compare_op=ALU.is_gt, fill=0.0, base=0,
                                   pattern=[[-1, P]], channel_multiplier=1).then_inc(const_ok, 1)
            pool.affine_select(out=upto[:], in_=upto[:], compare_op=ALU.is_ge, fill=0.0, base=0,
                               pattern=[[1, P]], channel_multiplier=-1).then_inc(const_ok, 1)
            for c in range(2):
                half = upto_c[c * C:(c + 1) * C]
                pool.wait_ge(const_ok, 4 + c)
                pool.affine_select(out=half, in_=half, compare_op=ALU.is_ge, fill=0.0, base=0,
                                   pattern=[[1, C]], channel_multiplier=-1).then_inc(const_ok, 1)
            pool.wait_ge(const_ok, 6)
            pool.memset(after_in[C:P, 0:C], 0.0).then_inc(const_ok, 1)
            pool.wait_ge(const_ok, 7)
            pool.memset(upto[0:C, C:P], 0.0).then_inc(const_ok, 1)
            pool.wait_ge(const_ok, 8)


            def low_fold(i):
                pool.wait_ge(foldraw_ok, i)
                pool.tensor_tensor(fold_lo[:], fold_raw[:], fold_hi[:].bitcast(F32), ALU.subtract).then_inc(fold_ok, 1)

            def add_y(p, pp):
                pool.wait_ge(y_read, p + 2)
                for h in range(2):
                    pool.wait_ge(y_ok, 2 * p + h + 1)
                    pool.tensor_tensor(yacc[:, pp], yacc[:, pp], y_new[:, h], ALU.add).then_inc(y_ok, 1)

            with pool.Fori(1, NKV - 1) as i:
                split_wqk(i + 1)
                low_fold(i)
                split_wvo(i, False)
                add_y(2 * i - 2, 0)
                add_y(2 * i - 1, 1)
            low_fold(NKV - 1)
            split_wvo(NKV - 1, False)
            add_y(2 * NKV - 4, 0)
            add_y(2 * NKV - 3, 1)

            pool.wait_ge(x1_ok, B)
            pool.wait_ge(var_ok, 2)
            pool.tensor_tensor(rstd[:], vare[:], mhalf[:], ALU.pow).then_inc(rstd_ok, 1)
            pool.memset(low_g[:], 1.0).then_inc(order_set, 1)
            pool.memset(comb3[:], 0.0).then_inc(order_set, 1)
            pool.wait_ge(a_ok, 1)
            pool.tensor_tensor(steps[:, 1], a_dt[:, 1].unsqueeze(2).broadcast_to([P, NH, C]),
                               upto_c[:].unsqueeze(1).broadcast_to([P, NH, C]), ALU.mult).then_inc(steps1_ok, 1)
            pool.wait_ge(order_set, 2)
            pool.memset(comb3[:, :, E], 1.0).then_inc(order_ok, 1)
            pool.affine_select(out=low_g[:], in_=low_g[:], compare_op=ALU.is_gt, fill=0.0, base=0,
                               pattern=[[1, G], [-1, G]], channel_multiplier=0).then_inc(order_ok, 1)
            for j in range(DI // P):
                pool.tensor_scalar(skip[:, j], ident[:], dskip[:, j:j + 1], 1.0, ALU.mult, ALU.mult).then_inc(skip_ok, 1)
            pool.wait_ge(vec_in, 16 * N_VEC)
            pool.wait_ge(wout_in, 16)
            for j in range(DI // P):
                pool.tensor_scalar(wout[:, j], wout[:, j], normw[:, j:j + 1], 1.0, ALU.mult, ALU.mult).then_inc(wout_ok, 1)
            pool.wait_ge(ends_ok, 1)
            for b in range(B):
                pool.wait_ge(xdt_ok, b + 1)
                for c in range(2):
                    rows_c = slice(0, (c + 1) * C)
                    pool.tensor_tensor(xq[rows_c, b, c], xdt[rows_c, b],
                                       ends[rows_c, 1 - c, b].unsqueeze(2).broadcast_to([(c + 1) * C, NH, HD]),
                                       ALU.mult).then_inc(xq_ok, 1)
            def low_pack(p, k):
                pool.wait_ge(packhi_ok, p + 1)
                pool.tensor_tensor(packs_lo[:, k], packs[:, k], packs_hi[:, k].bitcast(F32), ALU.subtract).then_inc(pack_ok, 1)

            for k in range(TPB):
                low_pack(k, k)
            pool.wait_ge(ss_ok, 1)
            pool.tensor_tensor(rinv[:], sse[:], mhalf[:], ALU.pow).then_inc(rinv_ok, 1)
            pool.wait_ge(var_ok, 3)
            pool.tensor_tensor(rstd[:], vare[:], mhalf[:], ALU.pow).then_inc(rstd_ok, 1)
            with pool.Fori(1, NM // TPB) as r:
                for k in range(TPB):
                    low_pack(TPB * r + k, k)
            for k in range(LAG):
                low_pack(NM + k, k)

        def pair_of(u):
            return u // 2

        @block.tensor
        def _(pe):
            def turn_tokens(src, done):
                for k in range(KT):
                    for b in range(B):
                        last = nc.tensor.transpose(tr_ps[:, 0, (k * B + b) * P:(k * B + b + 1) * P],
                                                   src[:, b, k * P:(k + 1) * P], ident[:])
                last.then_inc(done, 1)

            def split_products(dst, w_hi, w_lo, x_hi, x_lo, begins, ends):
                nc.tensor.matmul(dst, w_hi, x_hi, start=begins, stop=False)
                nc.tensor.matmul(dst, w_hi, x_lo, start=False, stop=False)
                return nc.tensor.matmul(dst, w_lo, x_hi, start=False, stop=ends)

            def project_q():
                for h in range(2):
                    for k in range(KT):
                        w, ts = slice(k * 2 * P + h * P, k * 2 * P + (h + 1) * P), slice(k * B * P, (k + 1) * B * P)
                        last = split_products(misc_ps[:, h * B * P:(h + 1) * B * P], wqk_hi[:, w], wqk_lo[:, w],
                                              xnT_hi[:, ts], xnT_lo[:, ts], k == 0, k == KT - 1)
                last.then_inc(q_ps, 1)

            def fold_k():
                split_products(misc_ps[:], wqk_hi[:, KT * 2 * P:], wqk_lo[:, KT * 2 * P:], qT_hi[:], qT_lo[:],
                               True, True).then_inc(qk_ps, 1)

            def fold_v():
                split_products(misc_ps[:], wvo_hi[:, 0:P], wvo_lo[:, 0:P], wvo_hi[:, P:], wvo_lo[:, P:],
                               True, True).then_inc(fold_ps, 1)

            def unit_scores(n, b, h, first):
                cols = slice(h * B * P + b * P, h * B * P + (b + 1) * P)
                for j in range(NB):
                    if not first:
                        pe.wait_ge(masked, 4 * n + (j - 3))
                    js = slice(j * BANK, (j + 1) * BANK)
                    nc.tensor.matmul(sc_ps[:, j], qk_hi[:, cols], ctxT_hi[b][:, js], start=True, stop=False)
                    nc.tensor.matmul(sc_ps[:, j], qk_hi[:, cols], ctxT_lo[b][:, js], start=False, stop=False)
                    nc.tensor.matmul(sc_ps[:, j], qk_lo[:, cols], ctxT_hi[b][:, js],
                                     start=False, stop=True).then_inc(scores, 1)

            def turn_probs(m, mu, g, first):
                if g == 0:
                    pe.wait_ge(exps, m + 1)
                if not (first and g < 2):
                    pe.wait_ge(turned_lo, 4 * m + (g - 1))
                for s in range(4):
                    t = 4 * g + s
                    last = nc.tensor.transpose(tr_ps[:, g % 2, s * P:(s + 1) * P],
                                               probs[:, mu % 2, t * P:(t + 1) * P], ident[:])
                last.then_inc(turned, 1)

            def pair_pv(pp, t):
                nc.tensor.matmul(pv_ps[:], ctx_hi[pp][:, t], pt[pp][:, t], start=(t == 0), stop=False)
                last = nc.tensor.matmul(pv_ps[:, 0:2 * P], ctx_lo[pp][:, t], pt[pp][:, t, 0:2 * P],
                                        start=False, stop=(t == ST - 1))
                if t == ST - 1:
                    last.then_inc(pv, 1)

            def pair_y():
                for h in range(2):
                    ts, ds = slice(h * P, (h + 1) * P), slice(h * D, (h + 1) * D)
                    last = split_products(misc_ps[:, ds], outT_hi[:, ts], outT_lo[:, ts], fold_hi[:, ds], fold_lo[:, ds],
                                          True, True)
                last.then_inc(y_ps, 1)

            def iteration(i, prev, more):
                for u in range(4):
                    n, b, h = 4 * i + u, u // 2, u % 2
                    if u == 0:
                        pe.wait_ge(qk_ok, i + 1)
                    if not prev and u == 0:
                        pe.wait_ge(split_T0, 3)
                    if not prev and u == 2:
                        pe.wait_ge(split_hi, 1)
                        pe.wait_ge(split_lo, 1)
                    unit_scores(n, b, h, not prev and u == 0)
                    if u == 0 and prev:
                        pe.wait_ge(wvo_split, i)
                        pe.wait_ge(qk_ok, i + 1)
                        pe.wait_ge(y_read, 2 * i - 1)
                        fold_v()
                    if u == 2 and more:
                        pe.wait_ge(wqk_split, i + 2)
                        if prev:
                            pe.wait_ge(y_read, 2 * i)
                        project_q()
                    if u == 3 and more:
                        pe.wait_ge(q_ok, i + 2)
                        fold_k()
                    for g in range(4):
                        if prev or u > 0:
                            turn_probs(n - 1, (u + 3) % 4, g, not prev and u == 1)
                        if g == 0 and u == 3:
                            pe.wait_ge(turned_lo, 16 * i + 8)
                            if prev:
                                pe.wait_ge(pv_read, 2 * i)
                            else:
                                pe.wait_ge(split_lo, 2)
                                pe.wait_ge(split_hi, 2)
                        if g == 0 and u == 1 and prev:
                            pe.wait_ge(turned_lo, 16 * i)
                            pe.wait_ge(pv_read, 2 * i - 1)
                            pe.wait_ge(split_lo, 3)
                        for t in ((0, 1), (2, 3, 4), (5,), (6, 7))[g]:
                            if u == 3:
                                pair_pv(0, t)
                            elif prev:
                                pair_pv(*((0, t + 8), (1, t), (1, t + 8))[u])
                        if g == 3 and u == 1 and prev:
                            pe.wait_ge(fold_ok, i)
                            pe.wait_ge(outT_ok, 2 * i - 1)
                            pair_y()
                        if g == 3 and u == 3 and prev:
                            pe.wait_ge(outT_ok, 2 * i)
                            if more:
                                pe.wait_ge(qk_ok, i + 2)
                            else:
                                pe.wait_ge(y_read, 2 * i)
                            pair_y()

            def keep_clock(bank, turns):
                for n in range(turns):
                    nc.tensor.transpose(bank[:, 0:P], ident[:], ident[:])

            pe.wait_ge(const_ok, 1)
            keep_clock(tr_ps[:, 1], WARM_START)
            pe.wait_ge(xn_ok, B)
            turn_tokens(xn, xnT_ps)
            pe.wait_ge(xnT_ok, 1)
            pe.wait_ge(wqk_split, 1)
            project_q()
            pe.wait_ge(q_ok, 1)
            fold_k()
            iteration(0, False, True)
            with pe.Fori(1, NKV - 1) as i:
                iteration(i, True, True)
            iteration(NKV - 1, True, False)
            for t in range(ST // 2, ST):
                pair_pv(0, t)
            pe.wait_ge(wvo_split, NKV)
            pe.wait_ge(y_read, 2 * NKV - 1)
            fold_v()
            for g in range(5):
                if g < 4:
                    turn_probs(4 * NKV - 1, 3, g, False)
                if g > 0:
                    pe.wait_ge(turned_lo, 16 * NKV - 4 + g)
                    if g == 1:
                        pe.wait_ge(pv_read, 2 * NKV - 1)
                    for t in range(4 * g - 4, 4 * g):
                        pair_pv(1, t)
                if g == 2:
                    pe.wait_ge(fold_ok, NKV)
                    pe.wait_ge(outT_ok, 2 * NKV - 1)
                    pair_y()
            keep_clock(tr_ps[:, 1], WARM_OUT)
            pe.wait_ge(outT_ok, 2 * NKV)
            pe.wait_ge(y_ok, 4 * NKV - 1)
            pair_y()

            keep_clock(tr_ps[:, 1], WARM_SSM)
            pe.wait_ge(xn_ok, 2 * B)
            turn_tokens(xn2, xnT_ps)
            keep_clock(tr_ps[:, 1], WARM_TURN)
            pe.wait_ge(xnT_ok, 2)
            pe.wait_ge(win_in, 16)
            for b in range(B):
                for k in range(KT):
                    last = nc.tensor.matmul(misc_ps[:, b * NH:(b + 1) * NH], x2T[:, k, b * P:(b + 1) * P],
                                            win[:, k, NI - NH:], start=(k == 0), stop=(k == KT - 1))
            last.then_inc(dt_ps, 1)
            for c in (2, 0, 1):
                for j in (2 * c, 2 * c + 1):
                    for k in range(KT):
                        last = nc.tensor.matmul(sc_ps[:, c, (j % 2) * B * P:(j % 2 + 1) * B * P],
                                                win[:, k, DI + j * P:DI + (j + 1) * P], x2T[:, k],
                                                start=(k == 0), stop=(k == KT - 1))
                last.then_inc(xbc_ps, 1)
            pe.wait_ge(const_ok, 8)
            pe.wait_ge(a_ok, 1)
            for k, tri in enumerate((after, after_in, upto)):
                last = nc.tensor.matmul(tr_ps[:, 1, k * B * NH:(k + 1) * B * NH], tri[:],
                                        a_dt[:].rearrange("p b h -> p (b h)"), start=True, stop=True)
            last.then_inc(ends_ps, 1)
            for b in range(B):
                if b == 0:
                    pe.wait_ge(steps0_ok, 1)
                else:
                    pe.wait_ge(steps1_ok, 1)
                    pe.wait_ge(ends_ok, 1)
                nc.tensor.matmul(tr_ps[:, b], after_in[:], steps[:, b].rearrange("p h t -> p (h t)"),
                                 start=True, stop=True).then_inc(seg_ps, 1)
            for b in range(B):
                for k in range(KT):
                    last = nc.tensor.matmul(sc_ps[:, 3] if b == 0 else pv_ps[:], x2T[:, k, b * P:(b + 1) * P],
                                            win[:, k, 0:DI], start=(k == 0), stop=(k == KT - 1))
                last.then_inc(z_ps, 1)
            pe.wait_ge(dt_abs, 1)
            keep_clock(misc_ps, WARM_CONV)
            pe.wait_ge(xc_ok, 1)
            for b in range(B):
                last = nc.tensor.matmul(misc_ps[:, b * P:(b + 1) * P], xc[:, 4, b], xc[:, 5, b], start=True, stop=True)
            last.then_inc(g_ps, 1)
            pe.wait_ge(xc_ok, 3)
            for b in range(B):
                for j in range(4):
                    last = nc.tensor.transpose(sc_ps[:, b, j * P:(j + 1) * P], xc[:, j, b], ident[:])
                last.then_inc(xh_ps, 1)
            pe.wait_ge(skip_ok, DI // P)
            pe.wait_ge(bc_ok, 1)
            for b in range(B):
                for j in range(DI // P):
                    nc.tensor.matmul((sc_ps[:, 2] if b == 0 else misc_ps[:])[:, j * P:(j + 1) * P], xc[:, j, b], skip[:, j],
                                     start=(j == 0), stop=False)
            for b in range(B):
                pe.wait_ge(mT_ok, b + 1)
                for h in range(NH):
                    last = nc.tensor.matmul((sc_ps[:, 2] if b == 0 else misc_ps[:])[:, h * HD:(h + 1) * HD],
                                            mT[:, b, h], xdt[:, b, h], start=False, stop=(h == NH - 1))
                last.then_inc(ssm_ps, 1)
                pe.wait_ge(sz_ok, b + 1)
                for c in range(2):
                    pe.wait_ge(xq_ok, 2 * b + c + 1)
                    rows_c = slice(0, (c + 1) * C)
                    last = nc.tensor.matmul((sc_ps[:, 3] if b == 0 else pv_ps[:])[c * C:(c + 1) * C],
                                            bc[rows_c, b, c * C:(c + 1) * C],
                                            xq[rows_c, b, c].rearrange("p h d -> p (h d)"), start=True, stop=True)
                last.then_inc(off_ps, 1)
            pe.wait_ge(decay_ok, 2)
            pe.wait_ge(wout_ok, DI // P)
            for b in range(B):
                pe.wait_ge(y2_ok, b + 1)
                for j in range(DI // P):
                    last = nc.tensor.transpose(tr_ps[:, b, j * P:(j + 1) * P], y2[:, b, j * P:(j + 1) * P], ident[:])
                last.then_inc(yT_ps, 1)
                keep_clock(sc_ps[:, b], WARM_TURN)
                pe.wait_ge(yT_ok, b + 1)
                for j in range(DI // P):
                    last = nc.tensor.matmul(sc_ps[:, b, 0:D], yT[:, b, j], wout[:, j], start=(j == 0), stop=(j == DI // P - 1))
                last.then_inc(o_ps, 1)

            keep_clock(tr_ps[:, 1], WARM_EXPERTS)
            pe.wait_ge(xn_ok, 3 * B)
            turn_tokens(xn3, xnT_ps)
            keep_clock(tr_ps[:, 1], WARM_TURN)
            pe.wait_ge(xnT_ok, 3)
            pe.wait_ge(vec_in, 16 * N_VEC)
            for b in range(B):
                for k in range(KT):
                    last = nc.tensor.matmul(pv_ps[:, b * E:(b + 1) * E], x3T[:, k, b * P:(b + 1) * P], gate[:, k],
                                            start=(k == 0), stop=(k == KT - 1))
            last.then_inc(gate_ps, 1)

            def hidden(m, k):
                pe.wait_ge(pack_ok, m + 1)
                for kt in range(KT):
                    w = slice(kt * P, (kt + 1) * P)
                    last = split_products(sc_ps[:, k, 0:B * P], packs_hi[:, k, w], packs_lo[:, k, w],
                                          x3T_hi[:, kt], x3T_lo[:, kt], kt == 0, kt == KT - 1)
                last.then_inc(h_ps, 1)

            def expert_tile(m, k, first, ahead=False):
                if not first and not ahead:
                    pe.wait_ge(h_act, m - 3)
                    hidden(m, k)
                if k >= LAG or not first:
                    pe.wait_ge(hc_ok, m - 1)
                nc.tensor.matmul(tr_ps[:, k % 2, 0:B * P], rows[:, bass.ds(m * P, P)], comb3T[:],
                                 start=True, stop=True).then_inc(c_ps, 1)
                if k >= LAG or not first:
                    expert_out(m, k, first and k == LAG, False)

            def expert_out(m, k, begins, ends):
                pe.wait_ge(h_ok, m - 1)
                for b in range(B):
                    ts, ks = slice(b * P, (b + 1) * P), (k - LAG) % TPB
                    last = split_products((pv_ps if b == 0 else misc_ps)[:, 0:D], hc_hi[:, ks, ts], hc_lo[:, ks, ts],
                                          packs_hi[:, k, KT * P:], packs_lo[:, k, KT * P:], begins, ends)
                    if ends and b == 0:
                        last.then_inc(first_whole, 1)
                last.then_inc(h_used, 1)

            pe.wait_ge(x2_ok, B)
            pe.wait_ge(x3_ok, 1)
            for k in range(TPB):
                hidden(k, k)
            keep_clock(misc_ps, WARM_PACKS)
            for k in range(LAG):
                pe.wait_ge(h_act, k + 1)
                hidden(TPB + k, k)
            keep_clock(misc_ps, WARM_GATE)
            pe.wait_ge(comb_ok, 1)
            for b in range(B):
                last = nc.tensor.transpose(misc_ps[0:W3, b * P:(b + 1) * P], comb3[:, b], ident[:])
            last.then_inc(combT_ps, 1)
            pe.wait_ge(combT_ok, 1)
            pe.wait_ge(rows_in, 16)
            for k in range(TPB):
                expert_tile(k, k, True)
            for k in range(TPB):
                expert_tile(TPB + k, k, False, k < LAG)
            with pe.Fori(2, NM // TPB) as r:
                for k in range(TPB):
                    expert_tile(TPB * r + k, k, False)
            for k in range(LAG):
                pe.wait_ge(pack_ok, NM + k + 1)
                expert_out(NM + k, k, False, k == LAG - 1)

        @block.scalar
        def _(act):
            def split_high(dst, src, arrived):
                act.wait_ge(arrived, 16)
                nc.scalar.copy(dst, src).then_inc(split_hi, 1)

            def iteration(i, prev, more):
                for u in range(4):
                    n = 4 * i + u
                    if u == 0 and prev:
                        act.wait_ge(fold_ps, i)
                        nc.scalar.copy(fold_hi[:], misc_ps[:]).then_inc(foldhi_ok, 1)
                    if u == 2 and more:
                        act.wait_ge(q_ps, i + 2)
                        nc.scalar.copy(qT_hi[:], misc_ps[:]).then_inc(qhi_ok, 1)
                    if u == 3 and more:
                        act.wait_ge(qk_ps, i + 2)
                        nc.scalar.copy(qk_hi[:], misc_ps[:]).then_inc(qkhi_ok, 1)
                    if u == 1 and prev:
                        high_outT(2 * i - 2)
                    if u == 3 and prev:
                        high_outT(2 * i - 1)
                    if u == 1 and not prev:
                        act.wait_ge(pen_ok, B)
                    if u == 3 and not prev:
                        act.wait_ge(split_lo, 3)
                        act.wait_ge(split_T0, 3)
                    if prev or u > 0:
                        high_parts(n - 1, (u + 3) % 4)
                    if not prev and u == 0:
                        split_high(ctxT_hi[1][:], ctxT_raw[1][:], ctxT_in[1])
                        split_high(ctx_hi[0][:], ctx_raw[0][:], ctx_in[0])
                    exponentials(n, u)
                    if u == 0 and prev:
                        nc.scalar.copy(fold_raw[:], misc_ps[:]).then_inc(foldraw_ok, 1)
                    if u == 1 and prev:
                        divide_y(2 * i - 2, 0)
                    if u == 3 and prev:
                        divide_y(2 * i - 1, 1)
                    if not prev and u < 2:
                        half = slice(u * ST // 2, (u + 1) * ST // 2)
                        split_high(ctx_hi[1][:, half], ctx_raw[1][:, half], ctx_in[1])

            def divide_y(p, pp):
                act.wait_ge(y_ps, p + 1)
                act.wait_ge(recips, p + 1)
                act.wait_ge(y_ok, 2 * p + 1)
                for h in range(2):
                    last = nc.scalar.activation(y_new[:, h], misc_ps[:, h * D:(h + 1) * D], ACT.Copy, scale=rz[:, pp, h:h + 1])
                last.then_inc(y_read, 1)

            def high_outT(p):
                act.wait_ge(pv_read, p + 1)
                nc.scalar.copy(outT_hi[:], outT[:]).then_inc(outThi_ok, 1)

            def high_parts(m, mu, blocks=range(4)):
                for g in blocks:
                    act.wait_ge(turned, 4 * m + (g + 1))
                    nc.scalar.copy(pt[mu // 2][:, 4 * g:4 * g + 4, (mu % 2) * P:(mu % 2 + 1) * P],
                                   tr_ps[:, g % 2].rearrange("p (s t) -> p s t", s=4)).then_inc(turned_hi, 1)

            def exponentials(n, u):
                act.wait_ge(negmax, n + 1)
                nc.scalar.activation(probs[:, u % 2], probs[:, u % 2], ACT.Exp, bias=nmax[:, u % 2:u % 2 + 1], scale=1.0,
                                     accum_out=zsum[:, u:u + 1]).then_inc(exps, 1)

            act.dma_start(wqk_sb[:], wqk[0]).then_inc(wqk_in, 16)
            nc.scalar.preload_act_table_set("natural_log_exp_and_others")
            act.wait_ge(wqk_in, 16)
            nc.scalar.copy(wqk_hi[:], wqk_sb[:]).then_inc(wqk_high, 1)
            act.wait_ge(xnT_ps, 1)
            nc.scalar.copy(xnT_hi[:], tr_ps[:, 0]).then_inc(xnThi_ok, 1)
            act.wait_ge(ctxT_in[0], 16)
            nc.scalar.copy(ctxT_hi[0][:], ctxT_raw[0][:]).then_inc(split_T0, 1)
            act.wait_ge(q_ps, 1)
            nc.scalar.copy(qT_hi[:], misc_ps[:]).then_inc(qhi_ok, 1)
            act.wait_ge(qk_ps, 1)
            nc.scalar.copy(qk_hi[:], misc_ps[:]).then_inc(qkhi_ok, 1)
            iteration(0, False, True)
            with act.Fori(1, NKV - 1) as i:
                iteration(i, True, True)
            iteration(NKV - 1, True, False)
            high_parts(4 * NKV - 1, 3, (0, 1))
            high_outT(2 * NKV - 2)
            act.wait_ge(fold_ps, NKV)
            nc.scalar.copy(fold_hi[:], misc_ps[:]).then_inc(foldhi_ok, 1)
            high_parts(4 * NKV - 1, 3, (2, 3))
            high_outT(2 * NKV - 1)
            act.wait_ge(vec_in, 16 * N_VEC)
            nc.scalar.activation(a_rate[:], alog, ACT.Exp).then_inc(ahead_exp, 1)

            act.wait_ge(xnT_ps, 2)
            nc.scalar.copy(x2T[:].rearrange("p k t -> p (k t)"), tr_ps[:, 0]).then_inc(xnT_ok, 1)
            act.wait_ge(dt_abs, 1)
            nc.scalar.activation(dtv[:, 4], dtv[:, 3], ACT.Exp).then_inc(dt_exp, 1)

            def first_tap(order, c):
                act.wait_ge(xbc_ps, order + 1)
                for j in (2 * c, 2 * c + 1):
                    last = nc.scalar.activation(conv[:, j], sc_ps[:, c].rearrange("p (j b t) -> p j b t", j=2, b=B)[:, j % 2],
                                                ACT.Identity, bias=convb[:, j:j + 1], scale=convw[:, j, CW - 1:CW])
                last.then_inc(tap0, 1)

            act.wait_ge(dt_one, 1)
            nc.scalar.activation(dtv[:, 8], dtv[:, 5], ACT.Ln).then_inc(dt_ln, 1)
            first_tap(0, 2)
            first_tap(1, 0)
            first_tap(2, 1)
            act.wait_ge(ends_ps, 1)
            nc.scalar.activation(ends[:].rearrange("p k b h -> p (k b h)"), tr_ps[:, 1, 0:3 * B * NH], ACT.Exp).then_inc(ends_ok, 1)
            for b in range(B):
                act.wait_ge(seg_ps, b + 1)
                nc.scalar.activation(decay[:, b].rearrange("p h t -> p (h t)"), tr_ps[:, b], ACT.Exp).then_inc(decay_ok, 1)
            nc.scalar.preload_act_table_set("silu_and_others")
            for order, c in enumerate((2, 0, 1)):
                act.wait_ge(taps, 6 * (order + 1))
                nc.scalar.activation(xc[:, 2 * c:2 * c + 2], conv[:, 2 * c:2 * c + 2], ACT.Silu).then_inc(xc_ok, 1)
            act.wait_ge(bcin_ok, 1)
            nc.scalar.copy(bc[:].rearrange("p b t -> p (b t)"), misc_ps[:, 0:B * P]).then_inc(bc_ok, 1)
            for b in range(B):
                act.wait_ge(z_ps, b + 1)
                nc.scalar.activation(sz[:, b], sc_ps[:, 3] if b == 0 else pv_ps[:], ACT.Silu).then_inc(sz_ok, 1)

            def high_pack(p, r, k):
                act.wait_ge(packs_in[k], 16 * r + 16)
                nc.scalar.copy(packs_hi[:, k], packs[:, k]).then_inc(packhi_ok, 1)

            for k in range(TPB):
                high_pack(k, 0, k)
            for b in range(B):
                act.wait_ge(y2_ok, b + 1)
                nc.scalar.activation(ysq[:, b], y2[:, b], ACT.Square, accum_out=ss[:, b:b + 1]).then_inc(sq_ok, 1)
                act.wait_ge(yT_ps, b + 1)
                nc.scalar.copy(yT[:, b].rearrange("p j t -> p (j t)"), tr_ps[:, b]).then_inc(yT_ok, 1)

            nc.scalar.preload_act_table_set("sigmoid_and_others")
            act.wait_ge(xnT_ps, 3)
            nc.scalar.copy(x3T[:].rearrange("p k t -> p (k t)"), tr_ps[:, 0]).then_inc(xnT_ok, 1)
            nc.scalar.copy(x3T_hi[:].rearrange("p k t -> p (k t)"), tr_ps[:, 0]).then_inc(x3hi_ok, 1)
            act.wait_ge(gate_ps, 1)
            nc.scalar.activation(sg[:].rearrange("p b e -> p (b e)"), pv_ps[:, 0:B * E], ACT.Sigmoid).then_inc(sg_ok, 1)

            def expert_act(m, k, first):
                act.wait_ge(h_ps, m + 1)
                if not first:
                    act.wait_ge(hc_ok, m - 3)
                nc.scalar.activation(hs[:, k], sc_ps[:, k, 0:B * P], ACT.Silu).then_inc(h_act, 1)

            for k in range(TPB):
                expert_act(k, k, True)
                if k >= TPB - LAG:
                    high_pack(k + LAG, 1, k + LAG - TPB)
            act.wait_ge(combT_ps, 1)
            nc.scalar.copy(comb3T[:], misc_ps[0:W3, 0:B * P]).then_inc(combT_ok, 1)
            act.wait_ge(h_used, 1)
            high_pack(TPB + 2, 1, 2)

            def expert_step(r, k, more):
                m = TPB * r + k
                expert_act(m, k, False)
                if more:
                    act.wait_ge(h_used, m - 2)
                    high_pack(m + 3, r if k == 0 else r + 1, (k + 3) % TPB)

            with act.Fori(1, NM // TPB - 1) as r:
                for k in range(TPB):
                    expert_step(r, k, True)
            for k in range(TPB):
                expert_step(NM // TPB - 1, k, k < TPB - 1)

        @block.vector
        def _(dve):
            def measure(src, b, turn):
                nc.vector.bn_stats(stats[:, b], src[:, b]).then_inc(bn_done, 1)
                dve.wait_ge(bn_done, B * (turn - 1) + b + 1)
                nc.vector.bn_aggr(mv[:, b], stats[:, b]).then_inc(mv_ok, 1)

            def normalise(dst, src, turn, first=0):
                for b in range(first, B):
                    measure(src, b, turn)
                dve.wait_ge(mv_ok, B * turn)
                nc.vector.tensor_scalar(vare[:], mv[:, :, 1], EPS, None, ALU.add).then_inc(var_ok, 1)
                dve.wait_ge(rstd_ok, turn)
                for b in range(B):
                    nc.vector.tensor_scalar(dst[:, b], src[:, b], mv[:, b, 0:1], rstd[:, b:b + 1],
                                            ALU.subtract, ALU.mult).then_inc(xn_ok, 1)

            def low_context(half):
                dve.wait_ge(split_T0, 1)
                cols = slice(half * S // 2, (half + 1) * S // 2)
                nc.vector.tensor_tensor(ctxT_lo[0][:, cols], ctxT_raw[0][:, cols], ctxT_hi[0][:, cols].bitcast(F32),
                                        ALU.subtract).then_inc(split_T0, 1)

            def penalties(b):
                nc.vector.tensor_scalar(pen[:, b], mask_u8[:, b], -1.0, -MASKED, ALU.add, ALU.mult).then_inc(pen_ok, 1)
                dve.wait_ge(pen_ok, b + 1)

            def valid(n, u):
                dve.wait_ge(negmax, n + 1)
                nc.vector.tensor_scalar(any_valid[:, u // 2:u // 2 + 1], nmax[:, u % 2:u % 2 + 1], -MASKED / 2, None,
                                        ALU.is_lt).then_inc(any_ok, 1)

            def take_outT(p):
                dve.wait_ge(pv, p + 1)
                nc.vector.tensor_reduce(outT[:], pv_ps[:].rearrange("p (z t) -> p t z", z=2), AX_X, ALU.add).then_inc(pv_read, 1)

            def take_y(p, pp):
                dve.wait_ge(y_ps, p + 1)
                dve.wait_ge(recips, p + 1)
                for h in range(2):
                    dve.wait_ge(y_ok, 2 * p + h + 1)
                    nc.vector.scalar_tensor_tensor(out=yacc[:, pp], in0=misc_ps[:, h * D:(h + 1) * D], scalar=rz[:, pp, h:h + 1],
                                                   in1=yacc[:, pp], op0=ALU.mult, op1=ALU.add).then_inc(y_ok, 1)

            def low_part(m, mu, g):
                dve.wait_ge(turned_hi, 4 * m + (g + 1))
                c = (mu % 2) * P
                t4 = slice(4 * g, 4 * g + 4)
                nc.vector.tensor_tensor(pt[mu // 2][:, t4, 2 * P + c:3 * P + c], tr_ps[:, g % 2].rearrange("p (s t) -> p s t", s=4),
                                        pt[mu // 2][:, t4, c:c + P].bitcast(F32), ALU.subtract).then_inc(turned_lo, 1)

            def low_copy(lo, src, hi, high, turn, done):
                dve.wait_ge(high, turn)
                nc.vector.tensor_tensor(lo[:], src, hi[:].bitcast(F32), ALU.subtract).then_inc(done, 1)

            def low_q(turn):
                low_copy(qk_lo, misc_ps[:], qk_hi, qkhi_ok, turn, qk_ok)

            def recip(p, pp, units):
                dve.wait_ge(exps, units)
                nc.vector.reciprocal(rz[:, pp], zsum[:, 2 * pp:2 * pp + 2]).then_inc(recips, 1)

            def iteration(i, prev, more):
                for u in range(4):
                    n, b = 4 * i + u, u // 2
                    if u == 1 and prev:
                        take_outT(2 * i - 2)
                    if u == 3 and prev:
                        take_outT(2 * i - 1)
                    for j in range(NB):
                        dve.wait_ge(scores, 4 * n + (j + 1))
                        nc.vector.memset(taker[:, j:j + 1], 0.0)
                        js = slice(j * BANK, (j + 1) * BANK)
                        nc.vector.tensor_tensor_reduce(probs[:, u % 2, js], sc_ps[:, j], pen[:, b, js], SCALE, -3e38,
                                                       ALU.add, ALU.max, mx[:, u % 2, j:j + 1]).then_inc(masked, 1)
                    dve.wait_ge(masked, 4 * n + 4)
                    nc.vector.tensor_reduce(nmax[:, u % 2:u % 2 + 1], mx[:, u % 2], AX_X, ALU.max, negate=True).then_inc(negmax, 1)
                    if u in (1, 3) and not more:
                        valid(n, u)
                    if u == 2 and more:
                        low_copy(qT_lo, misc_ps[:], qT_hi, qhi_ok, i + 2, q_ok)
                    if u == 3 and more:
                        low_q(i + 2)
                    for g in range(4):
                        if prev or u > 0:
                            low_part(n - 1, (u + 3) % 4, g)
                        if g == 1 and u in (1, 3) and prev:
                            low_copy(outT_lo, outT[:], outT_hi, outThi_ok, 2 * i - 1 + u // 2, outT_ok)
                    if u == 0 and prev:
                        recip(2 * i - 1, 1, 4 * i)
                    if u == 2:
                        recip(2 * i, 0, 4 * i + 2)

            nc.vector.memset(yacc[:], 0.0).then_inc(y_ok, 1)
            nc.vector.memset(y_new[:, 0, 0:1], 0.0).then_inc(y_read, 1)
            dve.wait_ge(x_in, 16)
            normalise(xn, x_sb, 1)
            low_copy(wqk_lo, wqk_sb[:], wqk_hi, wqk_high, 1, wqk_split)
            low_copy(xnT_lo, tr_ps[:, 0], xnT_hi, xnThi_ok, 1, xnT_ok)
            low_context(0)
            low_copy(qT_lo, misc_ps[:], qT_hi, qhi_ok, 1, q_ok)
            low_context(1)
            low_q(1)
            dve.wait_ge(mask_in, 16)
            penalties(0)
            penalties(1)
            iteration(0, False, True)
            with dve.Fori(1, NKV - 1) as i:
                iteration(i, True, True)
            iteration(NKV - 1, True, False)
            take_outT(2 * NKV - 2)
            for g in range(4):
                low_part(4 * NKV - 1, 3, g)
                if g == 1:
                    low_copy(outT_lo, outT[:], outT_hi, outThi_ok, 2 * NKV - 1, outT_ok)
                    low_copy(fold_lo, misc_ps[:], fold_hi, foldhi_ok, NKV, fold_ok)
            recip(2 * NKV - 1, 1, 4 * NKV)

            def add_attention(b):
                dve.wait_ge(y_ok, 4 * NKV - 1 + 2 * b)
                nc.vector.scalar_tensor_tensor(out=x1[:, b], in0=yacc[:, b], scalar=any_valid[:, b:b + 1], in1=x_sb[:, b],
                                               op0=ALU.mult, op1=ALU.add).then_inc(x1_ok, 1)
                dve.wait_ge(x1_ok, b + 1)

            dve.wait_ge(any_ok, B)
            take_y(2 * NKV - 2, 0)
            add_attention(0)
            measure(x1, 0, 2)
            take_outT(2 * NKV - 1)
            low_copy(outT_lo, outT[:], outT_hi, outThi_ok, 2 * NKV, outT_ok)
            take_y(2 * NKV - 1, 1)
            add_attention(1)

            done = [0]

            def link(ins):
                done[0] += 1
                ins.then_inc(dve_step, 1)
                dve.wait_ge(dve_step, done[0])

            normalise(xn2, x1, 2, 1)
            v, pos, neg, nab, e, u1, um, one, lnu, num, den, rec, q1, q2 = (dtv[:, k] for k in range(14))
            dve.wait_ge(dt_ps, 1)
            dve.wait_ge(vec_in, 16 * N_VEC)
            link(nc.vector.tensor_tensor(v, misc_ps[:, 0:B * NH].rearrange("p (b h) -> p b h", b=B),
                                         dtb.unsqueeze(1).broadcast_to([P, B, NH]), ALU.add))
            nc.vector.tensor_scalar(pos, v, 0.0, None, ALU.max)
            link(nc.vector.tensor_scalar(neg, v, 0.0, None, ALU.min))
            nc.vector.tensor_tensor(nab, neg, pos, ALU.subtract).then_inc(dt_abs, 1)

            def other_taps(order, c):
                dve.wait_ge(tap0, order + 1)
                for n in range(6):
                    j, k = 2 * c + n % 2, n // 2 + 1
                    if n >= 2:
                        dve.wait_ge(taps, 6 * order + n - 1)
                    nc.vector.scalar_tensor_tensor(
                        out=conv[:, j, :, k:], in0=sc_ps[:, c].rearrange("p (j b t) -> p j b t", j=2, b=B)[:, j % 2, :, 0:P - k],
                        scalar=convw[:, j, CW - 1 - k:CW - k], in1=conv[:, j, :, k:], op0=ALU.mult, op1=ALU.add).then_inc(taps, 1)

            dve.wait_ge(dt_exp, 1)
            link(nc.vector.tensor_scalar(u1, e, 1.0, None, ALU.add))
            nc.vector.tensor_scalar(um, u1, -1.0, None, ALU.add).then_inc(dt_one, 1)
            dve.wait_ge(dt_one, 1)
            link(nc.vector.tensor_scalar(one, um, 0.0, None, ALU.is_equal))
            link(nc.vector.tensor_tensor(den, um, one, ALU.add))
            link(nc.vector.reciprocal(rec, den))
            link(nc.vector.tensor_tensor(q1, rec, e, ALU.mult))
            dve.wait_ge(dt_ln, 1)
            link(nc.vector.tensor_tensor(num, lnu, one, ALU.add))
            link(nc.vector.tensor_tensor(q2, num, q1, ALU.mult))
            link(nc.vector.tensor_tensor(dt[:], pos, q2, ALU.add))
            dve.wait_ge(ahead_exp, 1)
            nc.vector.scalar_tensor_tensor(out=a_dt[:], in0=dt[:], scalar=-1.0, in1=a_rate[:].unsqueeze(1).broadcast_to([P, B, NH]),
                                           op0=ALU.mult, op1=ALU.mult).then_inc(a_ok, 1)
            dve.wait_ge(a_ok, 1)
            dve.wait_ge(const_ok, 8)
            nc.vector.tensor_tensor(steps[:, 0], a_dt[:, 0].unsqueeze(2).broadcast_to([P, NH, C]),
                                    upto_c[:].unsqueeze(1).broadcast_to([P, NH, C]), ALU.mult).then_inc(steps0_ok, 1)
            other_taps(0, 2)
            other_taps(1, 0)
            other_taps(2, 1)
            dve.wait_ge(g_ps, 1)
            nc.vector.tensor_tensor(bc_in[:], misc_ps[:, 0:B * P].rearrange("p (b t) -> p b t", b=B),
                                    upto[:].unsqueeze(1).broadcast_to([P, B, P]), ALU.mult).then_inc(bcin_ok, 1)

            def x_dt(b):
                dve.wait_ge(xh_ps, b + 1)
                nc.vector.tensor_tensor(xdt[:, b], sc_ps[:, b].rearrange("p (h d) -> p h d", h=NH),
                                        dt[:, b].unsqueeze(2).broadcast_to([P, NH, HD]), ALU.mult).then_inc(xdt_ok, 1)

            def decayed(b):
                dve.wait_ge(bcin_ok, 1)
                dve.wait_ge(decay_ok, b + 1)
                nc.vector.tensor_tensor(mT[:, b].rearrange("p h (c t) -> p h c t", c=2),
                                        decay[:, b].unsqueeze(2).broadcast_to([P, NH, 2, C]),
                                        bc_in[:, b].rearrange("p (c t) -> p c t", c=2).unsqueeze(1).broadcast_to([P, NH, 2, C]),
                                        ALU.mult).then_inc(mT_ok, 1)

            for b in range(B):
                x_dt(b)
                decayed(b)
            dve.wait_ge(ends_ok, 1)
            for b in range(B):
                dve.wait_ge(off_ps, b + 1)
                link(nc.vector.tensor_tensor(y_off[:, b], (sc_ps[:, 3] if b == 0 else pv_ps[:]).rearrange("p (h d) -> p h d", h=NH),
                                             ends[:, 2, b].unsqueeze(2).broadcast_to([P, NH, HD]), ALU.mult))
                dve.wait_ge(ssm_ps, b + 1)
                link(nc.vector.tensor_tensor(y1[:, b], sc_ps[:, 2] if b == 0 else misc_ps[:], y_off[:, b].rearrange("p h d -> p (h d)"), ALU.add))
                dve.wait_ge(sz_ok, b + 1)
                nc.vector.tensor_tensor(y2[:, b], y1[:, b], sz[:, b], ALU.mult).then_inc(y2_ok, 1)
            dve.wait_ge(sq_ok, B)
            nc.vector.tensor_scalar(sse[:], ss[:], 1.0 / DI, EPS, ALU.mult, ALU.add).then_inc(ss_ok, 1)
            dve.wait_ge(rinv_ok, 1)
            for b in range(B):
                dve.wait_ge(o_ps, b + 1)
                nc.vector.scalar_tensor_tensor(out=x2[:, b], in0=sc_ps[:, b, 0:D], scalar=rinv[:, b:b + 1],
                                               in1=x1[:, b], op0=ALU.mult, op1=ALU.add).then_inc(x2_ok, 1)
                dve.wait_ge(x2_ok, b + 1)
                if b == 0:
                    measure(x2, 0, 3)

            normalise(xn3, x2, 3, 1)
            dve.wait_ge(x3hi_ok, 1)
            nc.vector.tensor_tensor(x3T_lo[:].rearrange("p k t -> p (k t)"), tr_ps[:, 0],
                                    x3T_hi[:].rearrange("p k t -> p (k t)").bitcast(F32), ALU.subtract).then_inc(x3_ok, 1)
            dve.wait_ge(sg_ok, 1)
            sg4 = sg[:].rearrange("p b (g k) -> p (b g) k", k=E // G)
            nc.vector.tensor_tensor(pairs[:, :, 0:3], sg4[:, :, 0:3], sg4[:, :, 1:4], ALU.add)
            nc.vector.tensor_tensor(pairs[:, :, 3:5], sg4[:, :, 0:2], sg4[:, :, 2:4], ALU.add)
            link(nc.vector.tensor_tensor(pairs[:, :, 5:6], sg4[:, :, 0:1], sg4[:, :, 3:4], ALU.add))
            link(nc.vector.tensor_reduce(gsum[:].rearrange("p b g -> p (b g)"), pairs[:], AX_X, ALU.max))

            def two_best(val, n, low, cmp, rank, sel):
                mine = val[:].unsqueeze(3).broadcast_to([P, B, n, n])
                theirs = val[:].unsqueeze(2).broadcast_to([P, B, n, n])
                link(nc.vector.tensor_tensor(cmp[:, 0], theirs, mine, ALU.is_equal))
                for b in range(B):
                    last = nc.vector.tensor_tensor(cmp[:, 1, b], cmp[:, 0, b], low[:], ALU.mult)
                link(last)
                link(nc.vector.tensor_tensor(cmp[:, 2], theirs, mine, ALU.is_gt))
                link(nc.vector.tensor_tensor(cmp[:, 0], cmp[:, 2], cmp[:, 1], ALU.add))
                link(nc.vector.tensor_reduce(rank[:], cmp[:, 0], AX_X, ALU.add))
                link(nc.vector.tensor_scalar(sel[:], rank[:], 1.5, None, ALU.is_lt))

            dve.wait_ge(order_ok, 2)
            two_best(gsum, G, low_g, cmp_g, rank_g, sel_g)
            link(nc.vector.tensor_tensor(cand[:].rearrange("p b (g k) -> p (b g) k", k=E // G), sg4,
                                         sel_g[:].rearrange("p b g -> p (b g)").unsqueeze(2).broadcast_to([P, B * G, E // G]), ALU.mult))
            for turn in range(2):
                now = (cand if turn == 0 else others)[:]
                link(nc.vector.tensor_reduce(best[:, turn], now, AX_X, ALU.max))
                link(nc.vector.tensor_tensor(ties[:, turn], now, best[:, turn].unsqueeze(2).broadcast_to([P, B, E]), ALU.is_equal))
                link(nc.vector.tensor_tensor(placed[:, turn], ties[:, turn], places.unsqueeze(1).broadcast_to([P, B, E]), ALU.mult))
                link(nc.vector.tensor_reduce(place[:, turn], placed[:, turn], AX_X, ALU.max))
                link(nc.vector.tensor_tensor(picked[:, turn], placed[:, turn],
                                             place[:, turn].unsqueeze(2).broadcast_to([P, B, E]), ALU.is_equal))
                if turn == 0:
                    link(nc.vector.scalar_tensor_tensor(out=others[:], in0=picked[:, 0], scalar=-4.0, in1=cand[:],
                                                        op0=ALU.mult, op1=ALU.add))
            link(nc.vector.tensor_tensor(sel_e[:], picked[:, 0], picked[:, 1], ALU.add))
            link(nc.vector.tensor_tensor(wsel[:], cand[:], sel_e[:], ALU.mult))
            link(nc.vector.tensor_reduce(wsum[:], wsel[:], AX_X, ALU.add))
            link(nc.vector.tensor_scalar(wsum[:], wsum[:], 1e-20, None, ALU.add))
            link(nc.vector.reciprocal(wrec[:], wsum[:]))
            link(nc.vector.tensor_tensor(comb[:], wsel[:], wrec[:].unsqueeze(2).broadcast_to([P, B, E]), ALU.mult))
            link(nc.vector.tensor_copy(comb_hi[:], comb[:]))
            nc.vector.tensor_copy(comb3[:, :, 0:E], comb_hi[:])
            link(nc.vector.tensor_tensor(comb_rest[:], comb[:], comb_hi[:], ALU.subtract))
            link(nc.vector.tensor_copy(comb_mid[:], comb_rest[:]))
            nc.vector.tensor_copy(comb3[:, :, PART:PART + E], comb_mid[:])
            nc.vector.tensor_tensor(comb3[:, :, 2 * PART:2 * PART + E], comb_rest[:], comb_mid[:], ALU.subtract).then_inc(comb_ok, 1)

            def expert_weigh(m, k, first):
                dve.wait_ge(c_ps, m + 1)
                dve.wait_ge(h_act, m + 1)
                if not first:
                    dve.wait_ge(h_used, m - 3)
                nc.vector.tensor_tensor(hc[:, k], tr_ps[:, k % 2, 0:B * P], hs[:, k], ALU.mult).then_inc(hc_ok, 1)
                dve.wait_ge(hc_ok, m + 1)
                nc.vector.tensor_copy(hc_hi[:, k], hc[:, k]).then_inc(hchi_ok, 1)
                dve.wait_ge(hchi_ok, m + 1)
                nc.vector.tensor_tensor(hc_lo[:, k], hc[:, k], hc_hi[:, k].bitcast(F32), ALU.subtract).then_inc(h_ok, 1)

            for k in range(TPB):
                expert_weigh(k, k, True)
            with dve.Fori(1, NM // TPB) as r:
                for k in range(TPB):
                    expert_weigh(TPB * r + k, k, False)
            for b in range(B):
                if b == 0:
                    dve.wait_ge(first_whole, 1)
                else:
                    dve.wait_ge(h_used, NM)
                nc.vector.tensor_tensor(res[:, b], (pv_ps if b == 0 else misc_ps)[:, 0:D], x2[:, b], ALU.add).then_inc(res_ok, 1)


def kernel(x, ctx_1024, mask_BxS2_bf1, L0_xattn_Wq, L0_xattn_Wk, L0_xattn_Wv, L0_xattn_Wo, L0_attn_in_proj_w,
           L0_attn_conv_w, L0_attn_conv_b, L0_attn_A_log, L0_attn_D, L0_attn_dt_bias, L0_attn_norm_w,
           L0_attn_out_proj_w, L0_ffn_gate_w, L0_ffn_w1, L0_ffn_w2, L0_ffn_sw1, L0_ffn_sw2):
    import numpy as np
    import concourse.bacc as bacc
    from concourse.bass_utils import run_bass_kernel_spmd

    def flat(a):
        return np.ascontiguousarray(np.asarray(a))

    ctx = flat(ctx_1024)
    wq = flat(L0_xattn_Wq).reshape(KT, P, NKV, 2 * P).transpose(2, 1, 0, 3).reshape(NKV, P, KT * 2 * P)
    wk_t = flat(L0_xattn_Wk).reshape(P, NKV, P).transpose(1, 2, 0)
    wv_t = flat(L0_xattn_Wv).reshape(P, NKV, P).transpose(1, 2, 0)
    wo = flat(L0_xattn_Wo).reshape(NKV, 2, P, D).transpose(0, 2, 1, 3).reshape(NKV, P, 2 * D)
    w1 = np.concatenate([flat(L0_ffn_w1), flat(L0_ffn_sw1)]).transpose(1, 0, 2).reshape(D, (E + 1) * H)
    w1 = np.pad(w1, ((0, 0), (0, NM * P - (E + 1) * H))).reshape(KT, P, NM, P).transpose(2, 1, 0, 3)
    w2 = np.concatenate([flat(L0_ffn_w2), flat(L0_ffn_sw2)]).reshape((E + 1) * H, D)
    w2 = np.pad(w2, ((0, NM * P - (E + 1) * H), (0, 0))).reshape(NM, P, D)
    w_packs = np.zeros((NPK, P, KT * P + D), w1.dtype)
    w_packs[:NM, :, :KT * P] = w1.reshape(NM, P, KT * P)
    w_packs[LAG:, :, KT * P:] = w2
    expert_rows = np.zeros((W3, NM * P), np.uint16)
    for part in range(3):
        for e in range(E + 1):
            expert_rows[part * PART + e, e * H:(e + 1) * H] = 0x3F80

    small_by_row = np.concatenate([
        flat(L0_attn_conv_w).reshape(NX, P, CW).transpose(1, 0, 2).reshape(P, NX * CW), flat(L0_attn_conv_b).reshape(NX, P).T,
        flat(L0_attn_norm_w).reshape(DI // P, P).T, np.repeat(flat(L0_attn_D), HD).reshape(DI // P, P).T, flat(L0_ffn_gate_w).T.reshape(KT, P, E).transpose(1, 0, 2).reshape(P, KT * E),
        np.broadcast_to(np.arange(E, 0, -1, dtype=np.float32), (P, E)),
    ], axis=1)
    small_by_head = np.concatenate([flat(L0_attn_A_log), flat(L0_attn_dt_bias)])

    arrays = {
        "x": flat(x), "ctx": ctx, "ctx_t": ctx.transpose(0, 2, 1), "mask": flat(mask_BxS2_bf1).view(np.uint8),
        "wqk": np.concatenate([wq, wk_t], axis=2), "wvo": np.concatenate([wv_t, wo], axis=2),
        "win_t": flat(L0_attn_in_proj_w).T, "small_by_row": small_by_row, "small_by_head": small_by_head,
        "wout_t": flat(L0_attn_out_proj_w).T,
        "w_packs": w_packs, "expert_rows": expert_rows,
    }
    nc = bacc.Bacc("TRN2", target_bir_lowering=False, num_devices=1)
    arrays = {f"in_{name}": np.ascontiguousarray(a) for name, a in arrays.items()}
    args = [nc.dram_tensor(name, a.shape, mybir.dt.from_np(a.dtype), kind="ExternalInput").ap() for name, a in arrays.items()]
    out = nc.dram_tensor("out", (B, P, D), F32, kind="ExternalOutput").ap()
    cross_attention_ssm_moe(nc, *args, out)
    return run_bass_kernel_spmd(nc, [arrays], core_ids=[0]).results[0]["out"]
```
